# Optimizing a Trainium2 kernel written in Bass

```python
import numpy as np
import jax
import jax.numpy as jnp

def _softmax(x, axis=-1):
    return jax.nn.softmax(x, axis=axis)

def _gelu(x):
    return jax.nn.gelu(x, approximate=True)

def _silu(x):
    return jax.nn.silu(x)

def _sigmoid(x):
    return jax.nn.sigmoid(x)

def _layernorm(x, axis=-1, eps=1e-05):
    m = jnp.mean(x, axis=axis, keepdims=True)
    v = jnp.var(x, axis=axis, keepdims=True)
    return (x - m) / jnp.sqrt(v + eps)

def _scatter_add(tgt, idx, src, axis=0):
    return tgt.at[idx].add(src)

def _segment_sum(src, seg, n):
    return jax.ops.segment_sum(src, seg, n)
kernel_name = 'mk_gnn_resnorm_d4_gnn_r32_1c2ccd'

def setup_inputs(seed: int=0):
    np.random.seed(seed)
    _w = jnp.asarray

    def _rec_inputs():
        import jax
        import jax.numpy as jnp
        _gk = jax.random.key(seed)
        x = -0.000202 + 1 * jax.random.normal(jax.random.fold_in(_gk, 1), (50000, 64), jnp.float32)
        src = jax.random.randint(jax.random.fold_in(_gk, 2), (50000,), 0, 50000, jnp.int32)
        dst = jnp.minimum((50000 * jax.random.uniform(jax.random.fold_in(_gk, 3), (50000,)) ** 2.0).astype(jnp.int32), 49999)
        _o = jnp.argsort(dst, stable=True)
        src = src[_o]
        dst = dst[_o]
        edge_type_8 = jax.random.randint(jax.random.fold_in(_gk, 13), (50000,), 0, 8, jnp.int32)
        edge_weight1 = jax.random.uniform(jax.random.fold_in(_gk, 14), (50000, 1), jnp.float32, 0.0, 0.999999)
        return (x, src, dst, edge_type_8, edge_weight1)
    x, src, dst, edge_type_8, edge_weight1 = _rec_inputs()

    def _L0_gnn_setup():
        import jax, jax.numpy as jnp
        import numpy as np
        N_NODES = 3125
        N_EDGES = 50000
        D_FEAT = 64
        key = jax.random.key(seed)
        k1, k2 = jax.random.split(key)
        x = jax.random.normal(k1, (N_NODES, D_FEAT), dtype=jnp.float32)
        edge_index = jax.random.randint(k2, (2, N_EDGES), 0, N_NODES, dtype=jnp.int64)
        return {'x': x, 'edge_index': edge_index}
    _L0_gnn_all = _L0_gnn_setup()
    _L0_gnn_in = {k: v for k, v in _L0_gnn_all.items() if k in ()}
    del _L0_gnn_all

    def _L1_gnn_setup():
        import jax, jax.numpy as jnp
        import numpy as np
        N_NODE = 50000
        N_EDGE = 31250
        IN_CH = 64
        HID_CH = 64
        NUM_REL = 8
        key = jax.random.key(seed)
        k1, k2, k3, k4 = jax.random.split(key, 4)
        x = jax.random.normal(k1, (N_NODE, IN_CH), dtype=jnp.float32)
        W = jax.random.normal(k2, (NUM_REL, IN_CH, HID_CH), dtype=jnp.float32)
        edge_index = jax.random.randint(k3, (2, N_EDGE), 0, N_NODE, dtype=jnp.int64)
        rel = jax.random.randint(k4, (N_EDGE,), 0, NUM_REL, dtype=jnp.int64)
        return {'x': x, 'W': W, 'edge_index': edge_index, 'rel': rel, 'num_node': N_NODE, 'num_edge': N_EDGE}
    _L1_gnn_all = _L1_gnn_setup()
    _L1_gnn_in = {k: v for k, v in _L1_gnn_all.items() if k in ('W',)}
    del _L1_gnn_all

    def _L2_gnn_setup():
        import jax, jax.numpy as jnp
        import numpy as np
        N_NODES = 50000
        N_EDGES = 25000
        NODE_NF = 64
        HIDDEN_NF = 128

        def _linear_params(key, fan_in, fan_out):
            kw, kb = jax.random.split(key)
            bound = 1.0 / np.sqrt(fan_in)
            W = jax.random.uniform(kw, (fan_in, fan_out), minval=-bound, maxval=bound, dtype=jnp.float32)
            b = jax.random.uniform(kb, (fan_out,), minval=-bound, maxval=bound, dtype=jnp.float32)
            return (W, b)
        key = jax.random.key(seed)
        ks = jax.random.split(key, 8)
        h = jax.random.normal(ks[0], (N_NODES, NODE_NF), dtype=jnp.float32)
        row = jax.random.randint(ks[1], (N_EDGES,), 0, N_NODES)
        col = jax.random.randint(ks[2], (N_EDGES,), 0, N_NODES)
        dist = jax.random.uniform(ks[3], (N_EDGES, 1), dtype=jnp.float32)
        eW1, eb1 = _linear_params(ks[4], 2 * NODE_NF + 1, HIDDEN_NF)
        eW2, eb2 = _linear_params(ks[5], HIDDEN_NF, HIDDEN_NF)
        nW1, nb1 = _linear_params(ks[6], HIDDEN_NF + NODE_NF, HIDDEN_NF)
        nW2, nb2 = _linear_params(ks[7], HIDDEN_NF, NODE_NF)
        return {'h': h, 'row': row, 'col': col, 'dist': dist, 'eW1': eW1, 'eb1': eb1, 'eW2': eW2, 'eb2': eb2, 'nW1': nW1, 'nb1': nb1, 'nW2': nW2, 'nb2': nb2}
    _L2_gnn_all = _L2_gnn_setup()
    _L2_gnn_in = {k: v for k, v in _L2_gnn_all.items() if k in ('eW1', 'eb1', 'eW2', 'eb2', 'nW1', 'nb1', 'nW2', 'nb2')}
    del _L2_gnn_all

    def _L3_gnn_setup():
        import jax, jax.numpy as jnp
        import numpy as np
        N = 3125
        E = 50000
        D = 64

        def _gcn_conv(x, src, dst, W, b, n):
            h = x @ W
            deg = jax.ops.segment_sum(jnp.ones(src.shape, x.dtype), dst, num_segments=n)
            dinv = jnp.where(deg > 0, jax.lax.rsqrt(deg), 0.0)
            norm = dinv[src] * dinv[dst]
            msg = h[src] * norm[:, None]
            return jax.ops.segment_sum(msg, dst, num_segments=n) + b
        key = jax.random.key(seed)
        ks = jax.random.split(key, 8)
        s = 1.0 / np.sqrt(D)
        return {'x': jax.random.normal(ks[0], (N, D), dtype=jnp.float32), 'edge_index': jax.random.randint(ks[1], (2, E), 0, N, dtype=jnp.int32), 'W1': jax.random.normal(ks[2], (D, D), dtype=jnp.float32) * s, 'b1': jnp.zeros((D,), dtype=jnp.float32), 'W2': jax.random.normal(ks[3], (D, D), dtype=jnp.float32) * s, 'b2': jnp.zeros((D,), dtype=jnp.float32), 'W_emb': jax.random.normal(ks[4], (D, D), dtype=jnp.float32) * s, 'b_emb': jnp.zeros((D,), dtype=jnp.float32)}
    _L3_gnn_all = _L3_gnn_setup()
    _L3_gnn_in = {k: v for k, v in _L3_gnn_all.items() if k in ('W1', 'b1', 'W2', 'b2', 'W_emb', 'b_emb')}
    del _L3_gnn_all
    return {'x': x, 'src': src, 'dst': dst, 'edge_type_8': edge_type_8, 'edge_weight1': edge_weight1, 'L1_gnn_W': _L1_gnn_in['W'], 'L2_gnn_eW1': _L2_gnn_in['eW1'], 'L2_gnn_eb1': _L2_gnn_in['eb1'], 'L2_gnn_eW2': _L2_gnn_in['eW2'], 'L2_gnn_eb2': _L2_gnn_in['eb2'], 'L2_gnn_nW1': _L2_gnn_in['nW1'], 'L2_gnn_nb1': _L2_gnn_in['nb1'], 'L2_gnn_nW2': _L2_gnn_in['nW2'], 'L2_gnn_nb2': _L2_gnn_in['nb2'], 'L3_gnn_W1': _L3_gnn_in['W1'], 'L3_gnn_b1': _L3_gnn_in['b1'], 'L3_gnn_W2': _L3_gnn_in['W2'], 'L3_gnn_b2': _L3_gnn_in['b2'], 'L3_gnn_W_emb': _L3_gnn_in['W_emb'], 'L3_gnn_b_emb': _L3_gnn_in['b_emb']}

def reference(x, src, dst, edge_type_8, edge_weight1, L1_gnn_W, L2_gnn_eW1, L2_gnn_eb1, L2_gnn_eW2, L2_gnn_eb2, L2_gnn_nW1, L2_gnn_nb1, L2_gnn_nW2, L2_gnn_nb2, L3_gnn_W1, L3_gnn_b1, L3_gnn_W2, L3_gnn_b2, L3_gnn_W_emb, L3_gnn_b_emb):
    import jax
    import jax.numpy as jnp

    def _L0_gnn_ref(x, edge_index):
        import jax, jax.numpy as jnp
        import numpy as np
        N_NODES = 3125
        N_EDGES = 50000
        D_FEAT = 64
        row, col = (edge_index[0], edge_index[1])
        n = x.shape[0]
        deg = jax.ops.segment_sum(jnp.ones(row.shape[0], dtype=x.dtype), row, num_segments=n)
        deg_inv_sqrt = jnp.where(deg > 0, jax.lax.rsqrt(jnp.maximum(deg, 1.0)) * jnp.where(deg > 0, 1.0, 0.0), 0.0)
        deg_inv_sqrt = jnp.where(deg > 0, jax.lax.rsqrt(jnp.maximum(deg, 1.0)), 0.0)
        norm = deg_inv_sqrt[row] * deg_inv_sqrt[col]
        msgs = x[col] * norm[:, None]
        out = jax.ops.segment_sum(msgs, row, num_segments=n)
        return out

    def _L1_gnn_ref(x, W, edge_index, rel, num_node, num_edge):
        import jax, jax.numpy as jnp
        import numpy as np
        N_NODE = 50000
        N_EDGE = 31250
        IN_CH = 64
        HID_CH = 64
        NUM_REL = 8
        src = edge_index[0, :num_edge]
        dst = edge_index[1, :num_edge]
        r = rel[:num_edge]
        xw = jnp.einsum('ni,rih->rnh', x, W)
        transformed = xw[r, src]
        out = jax.ops.segment_sum(transformed, dst, num_segments=num_node)
        return out

    def _L2_gnn_ref(h, row, col, dist, eW1, eb1, eW2, eb2, nW1, nb1, nW2, nb2):
        import jax, jax.numpy as jnp
        import numpy as np
        N_NODES = 50000
        N_EDGES = 25000
        NODE_NF = 64
        HIDDEN_NF = 128

        def _linear_params(key, fan_in, fan_out):
            kw, kb = jax.random.split(key)
            bound = 1.0 / np.sqrt(fan_in)
            W = jax.random.uniform(kw, (fan_in, fan_out), minval=-bound, maxval=bound, dtype=jnp.float32)
            b = jax.random.uniform(kb, (fan_out,), minval=-bound, maxval=bound, dtype=jnp.float32)
            return (W, b)
        edge_in = jnp.concatenate([h[row], h[col], dist], axis=1)
        e = jax.nn.silu(edge_in @ eW1 + eb1)
        e = jax.nn.silu(e @ eW2 + eb2)
        agg = jax.ops.segment_sum(e, row, num_segments=h.shape[0])
        node_in = jnp.concatenate([h, agg], axis=1)
        out = jax.nn.silu(node_in @ nW1 + nb1) @ nW2 + nb2
        return out

    def _L3_gnn_ref(x, edge_index, W1, b1, W2, b2, W_emb, b_emb):
        import jax, jax.numpy as jnp
        import numpy as np
        N = 3125
        E = 50000
        D = 64

        def _gcn_conv(x, src, dst, W, b, n):
            h = x @ W
            deg = jax.ops.segment_sum(jnp.ones(src.shape, x.dtype), dst, num_segments=n)
            dinv = jnp.where(deg > 0, jax.lax.rsqrt(deg), 0.0)
            norm = dinv[src] * dinv[dst]
            msg = h[src] * norm[:, None]
            return jax.ops.segment_sum(msg, dst, num_segments=n) + b
        n = x.shape[0]
        loop = jnp.arange(n, dtype=edge_index.dtype)
        src = jnp.concatenate([edge_index[0], loop])
        dst = jnp.concatenate([edge_index[1], loop])
        h = jax.nn.relu(_gcn_conv(x, src, dst, W1, b1, n))
        out = _gcn_conv(h, src, dst, W2, b2, n)
        return out + (x @ W_emb + b_emb)
    edge_index = jnp.stack([src, dst])
    x = _layernorm(x + _L0_gnn_ref(x, edge_index), axis=-1)
    x = _layernorm(x + _L1_gnn_ref(x, L1_gnn_W, edge_index, edge_type_8, 50000, 50000), axis=-1)
    x = _layernorm(x + _L2_gnn_ref(x, src, dst, edge_weight1, L2_gnn_eW1, L2_gnn_eb1, L2_gnn_eW2, L2_gnn_eb2, L2_gnn_nW1, L2_gnn_nb1, L2_gnn_nW2, L2_gnn_nb2), axis=-1)
    x = _layernorm(x + _L3_gnn_ref(x, edge_index, L3_gnn_W1, L3_gnn_b1, L3_gnn_W2, L3_gnn_b2, L3_gnn_W_emb, L3_gnn_b_emb), axis=-1)
    return x

_drawn_inputs = setup_inputs


def setup_inputs(seed=0):
    import zlib

    import numpy as np

    out = dict(_drawn_inputs(seed))
    spreads = {'L3_gnn_b1': (0.0, 0.1), 'L3_gnn_b2': (0.0, 0.1), 'L3_gnn_b_emb': (0.0, 0.1)}
    factors = {'edge_weight1': 8.0,
     'L2_gnn_eW1': 3.441,
     'L2_gnn_eb1': 8.0,
     'L2_gnn_eW2': 3.321,
     'L2_gnn_eb2': 8.0,
     'L2_gnn_nb1': 4.553}
    for name, (base, spread) in spreads.items():
        noise = np.random.default_rng([zlib.crc32(name.encode()), seed]).standard_normal(out[name].shape)
        drawn = base * np.exp(spread * noise) if base else spread * noise
        out[name] = jnp.asarray(drawn.astype(out[name].dtype))
    for name, factor in factors.items():
        out[name] = (out[name] * factor).astype(out[name].dtype)
    return out
```

```python
import numpy as np
import concourse.bass as bass
from concourse import mybir
from contextlib import ExitStack

F32 = mybir.dt.float32
F16 = mybir.dt.float16
I32 = mybir.dt.int32
ALU = mybir.AluOpType
ACT = mybir.ActivationFunctionType
AX = mybir.AxisListType

P = 128
N = 50000
D = 64
HID = 128
REL = 8
QUAD = 4
QUADS = 98
ROUNDS = QUADS // 2
QE = QUAD * P
FULLQ = N // QE
RESTQ = N - FULLQ * QE
T = QUADS * QUAD
NR = P * T
PADKEY = NR - 1
NA = NR + P
CH = 28
CHUNKS = T // CH
CROUNDS = CHUNKS // 2
CW = CH * D
LASTP = P - 1
LASTT = N - LASTP * T
EPS = 1e-5


def bc(ap, shape):
    return ap.to_broadcast(shape)


def flip128(nc, out, a, ident):
    return nc.tensor.matmul(out, a, ident, is_transpose=True, start=True, stop=True)


def clear(nc, sems):
    with nc.Block() as block:
        @block.gpsimd
        def _(pool):
            for s in sems:
                pool.sem_clear(s)


def rounds(eng, count, body):
    body(0, True, False)
    with eng.Fori(1, count - 1) as i:
        body(i, False, False)
    body(count - 1, False, True)


def chunk_of(table, c):
    return table[0:NR, :].rearrange("(p t) f -> p (t f)", p=P)[:, bass.ds(c * CW, CW)]


def edge_pass(nc, label, K, sources, key, sums, width, kind, zero=None, weights=None):
    ng = len(sources)
    nt = len(sums)
    with ExitStack() as ctx:
        def sb(name, shape, dt=F32):
            return ctx.enter_context(nc.sbuf_tensor(f"{label}_{name}", shape, dt))

        def ps(name, shape):
            return ctx.enter_context(nc.psum_tensor(f"{label}_{name}", shape, F32))

        sems = []

        def sem(name):
            sems.append(K["semaphore"](f"edge_{name}"))
            return sems[-1]

        def own_sem(name):
            return K["semaphore"](f"{label}_{name}")

        gidx = [[sb(f"gidx{g}_{h}", [P, QUAD], I32) for h in range(2)] for g in range(ng)]
        rows = [sb(f"rows{h}", [P, QUAD, D * ng]) for h in range(2)]
        keys = [sb(f"keys{h}", [P, QUAD]) for h in range(2)]
        same = [sb(f"same{h}", [P, QUAD, P]) for h in range(2)]
        sidx = [sb(f"sidx{h}", [P, QUAD], I32) for h in range(2)]
        total = [sb(f"total{h}", [P, QUAD, width]) for h in range(2)]
        earlier = sb("earlier", [P, QUAD])
        scratch = sb("scratch", [P, P])
        away = sb("away", [P, QUAD])
        step = sb("step", [P, QUAD])
        p_key = [ps(f"p_key{h}", [P, QUAD, P]) for h in range(2)]
        p_sum = [ps(f"p_sum{h}", [P, QUAD, P]) for h in range(2)]

        s_gidx = sem("gidx")
        s_rows = [own_sem(f"rows{h}") for h in range(2)]
        s_keys = sem("keys")
        s_prow = sem("prow")
        s_same = sem("same")
        s_cnt = sem("cnt")
        s_sidx = sem("sidx")
        s_sum = sem("sum")
        s_total = sem("total")
        s_added = [own_sem(f"added{j}") for j in range(QUAD)]
        s_zero = sem("zero")
        s_turn = sem("turn")
        if kind == "rel":
            s_mask = sem("mask")
            s_z = sem("z")
            s_zt = sem("zt")
            s_ztb = sem("ztb")
            mask = [sb(f"mask{h}", [P, QUAD, REL]) for h in range(2)]
            z = [sb(f"z{h}", [P, REL, D]) for h in range(2)]
            ztb = [sb(f"ztb{h}", [P, QUAD, P]) for h in range(2)]
            p_zt = [ps(f"p_zt{h}", [P, QUAD, P]) for h in range(2)]
        if kind == "mlp":
            s_ew = [sem(f"ew{h}") for h in range(2)]
            s_pt = sem("pt")
            s_ht = sem("ht")
            s_p1 = sem("p1")
            s_e1 = sem("e1")
            s_p2 = sem("p2")
            s_e2 = sem("e2")
            ew = [sb(f"ew{h}", [1, QE]) for h in range(2)]
            ht = sb("ht", [P, QE])
            e1 = sb("e1", [P, QE])
            e2 = sb("e2", [P, QUAD, HID])
            p_t = ps("p_t", [P, QE])
            p_1 = ps("p_1", [P, QE])
            p_2 = ps("p_2", [P, QUAD, HID])
        inner = ctx.enter_context(ExitStack())
        block = inner.enter_context(nc.Block())

        def scattered(eng, q):
            for j in range(QUAD):
                eng.wait_ge(s_added[j], 16 * (q - 1))

        @block.sync
        def _(sp):
            if kind == "mlp":
                ew_rows = weights["ew"]

                def body(i, first, last):
                    for h in range(2):
                        q = i * 2 + h
                        if not first:
                            sp.wait_ge(s_p1, q - 1)
                        if last and h == 1:
                            sp.dma_start(ew[h][0:1, 0:RESTQ],
                                         ew_rows[FULLQ * QE:N].rearrange("(a n) -> a n", a=1)
                                         ).then_inc(s_ew[h], 16)
                        else:
                            sp.dma_start(ew[h][0:1, :],
                                         ew_rows[bass.ds(q * QE, QE)].rearrange("(a n) -> a n", a=1)
                                         ).then_inc(s_ew[h], 16)
            if zero:
                tile, tables, piece = zero
                n = 0
                for table in tables:
                    flat = table.rearrange("(p t) f -> p (t f)", p=P)
                    for a in range(0, flat.shape[1], piece):
                        sp.dma_start(flat[:, a:a + piece], tile[:, 0:piece]).then_inc(s_zero, 16)
                        n += 1
                sp.wait_ge(s_zero, 16 * n)
            if kind == "mlp":
                rounds(sp, ROUNDS, body)

        @block.gpsimd
        def _(pool):
            def gather(h):
                for j in range(QUAD):
                    for g, (table, _) in enumerate(sources):
                        pool.indirect_dma_start(
                            out=rows[h][:, j, g * D:(g + 1) * D], out_offset=None, in_=table,
                            in_offset=bass.IndirectOffsetOnAxis(ap=gidx[g][h][:, j:j + 1], axis=0)
                        ).then_inc(s_rows[h], 16)

            for h in range(2):
                pool.wait_ge(s_gidx, h + 1)
                gather(h)

            def body(i, first, last):
                for h in range(2):
                    q = i * 2 + h
                    pool.wait_ge(s_sidx, q + 1)
                    pool.wait_ge(s_total, q + 1)
                    if not last:
                        pool.wait_ge(s_gidx, q + 3)
                    for j in range(QUAD):
                        if j >= nt:
                            pool.wait_ge(s_added[j - nt], 16 * (q + 1))
                        elif not (first and h == 0):
                            pool.wait_ge(s_added[j - nt + QUAD], 16 * q)
                        pool.sem_inc(s_turn, 1)
                        pool.indirect_dma_start(
                            out=sums[j % nt],
                            out_offset=bass.IndirectOffsetOnAxis(ap=sidx[h][:, j:j + 1], axis=0),
                            in_=total[h][:, j, :], in_offset=None, compute_op=ALU.add
                        ).then_inc(s_added[j], 16)
                        if not last:
                            for g, (table, _) in enumerate(sources):
                                pool.indirect_dma_start(
                                    out=rows[h][:, j, g * D:(g + 1) * D], out_offset=None, in_=table,
                                    in_offset=bass.IndirectOffsetOnAxis(ap=gidx[g][h][:, j:j + 1], axis=0)
                                ).then_inc(s_rows[h], 16)

            rounds(pool, ROUNDS, body)
            for j in range(QUAD):
                pool.wait_ge(s_added[j], 16 * QUADS)

        landed = 16 * QUAD * ng

        @block.vector
        def _(dve):
            def stage_gather(q, h):
                for g, (_, index) in enumerate(sources):
                    last = nc.vector.tensor_copy(gidx[g][h][:, :], index[:, :, q])
                last.then_inc(s_gidx, 1)

            for h in range(2):
                stage_gather(h, h)
            nc.vector.tensor_copy(keys[0][:, :], key[:, :, 0]).then_inc(s_keys, 1)

            def body(i, first, last):
                for h in range(2):
                    q = i * 2 + h
                    if not (last and h == 1):
                        if not (first and h == 0):
                            dve.wait_ge(s_prow, q)
                            dve.wait_ge(s_sidx, q)
                        nc.vector.tensor_copy(keys[1 - h][:, :], key[:, :, q + 1]).then_inc(s_keys, 1)
                    dve.wait_ge(s_prow, q + 1)
                    dve.wait_ge(s_keys, q + 1)
                    if not first:
                        dve.wait_ge(s_sum, q - 1)
                    nc.vector.tensor_tensor(same[h][:, :, :], p_key[h][:, :, :],
                                            bc(keys[h][:, :].unsqueeze(2), [P, QUAD, P]),
                                            ALU.is_equal).then_inc(s_same, 1)
                    dve.wait_ge(s_same, q + 1)
                    for j in range(QUAD):
                        if j:
                            dve.wait_ge(s_cnt, q * 6 + j)
                        nc.vector.tensor_tensor_reduce(
                            out=scratch[:, :], in0=same[h][:, j, :], in1=K["before"][:, :], scale=1.0,
                            scalar=0.0, op0=ALU.mult, op1=ALU.add, accum_out=earlier[:, j:j + 1]
                        ).then_inc(s_cnt, 1)
                    nc.vector.tensor_scalar(away[:, :], keys[h][:, :], -1.0, K["spare"][:, 0:1],
                                            ALU.mult, ALU.add).then_inc(s_cnt, 1)
                    dve.wait_ge(s_cnt, q * 6 + 5)
                    nc.vector.scalar_tensor_tensor(out=step[:, :], in0=earlier[:, :], scalar=0.5,
                                                   in1=away[:, :], op0=ALU.is_gt, op1=ALU.mult
                                                   ).then_inc(s_cnt, 1)
                    dve.wait_ge(s_cnt, q * 6 + 6)
                    if not first:
                        scattered(dve, q)
                    nc.vector.tensor_tensor(sidx[h][:, :], step[:, :], keys[h][:, :], ALU.add
                                            ).then_inc(s_sidx, 1)
                    dve.wait_ge(s_rows[h], (i + 1) * landed)
                    if not last:
                        stage_gather(q + 2, h)
                    if kind == "rel":
                        if not first:
                            dve.wait_ge(s_zt, 4 * q - 4)
                        nc.vector.tensor_tensor(mask[h][:, :, :],
                                                bc(K["iota"][:, 0:REL].unsqueeze(1), [P, QUAD, REL]),
                                                bc(K["rel"][:, :, q].unsqueeze(2), [P, QUAD, REL]),
                                                ALU.is_equal).then_inc(s_mask, 1)
                        dve.wait_ge(s_mask, q + 1)
                        for j in range(QUAD):
                            if not (first and h == 0 and j < 2):
                                dve.wait_ge(s_zt, 4 * q + j - 1)
                            nc.vector.tensor_tensor(z[j % 2][:, :, :],
                                                    bc(rows[h][:, j, :].unsqueeze(1), [P, REL, D]),
                                                    bc(mask[h][:, j, :].unsqueeze(2), [P, REL, D]),
                                                    ALU.mult).then_inc(s_z, 1)
                    if kind == "mlp":
                        dve.wait_ge(s_sum, q + 1)
                        nc.vector.tensor_copy(total[h][:, :, :], p_sum[h][:, :, 0:width]).then_inc(s_total, 1)

            rounds(dve, ROUNDS, body)

        @block.tensor
        def _(pe):
            def spread(h):
                for j in range(QUAD):
                    last = nc.tensor.matmul(p_key[h][:, j, :], bc(keys[h][:, j:j + 1], [P, P]),
                                            K["ident"][:, :], start=True, stop=True)
                last.then_inc(s_prow, 1)

            pe.wait_ge(s_keys, 1)
            spread(0)

            def body(i, first, last):
                for h in range(2):
                    q = i * 2 + h
                    if not (last and h == 1):
                        pe.wait_ge(s_keys, q + 2)
                        if not (first and h == 0):
                            pe.wait_ge(s_same, q)
                        spread(1 - h)
                    pe.wait_ge(s_rows[h], (i + 1) * landed)
                    if kind == "mlp":
                        if not (first and h == 0):
                            pe.wait_ge(s_ht, q)
                        for j in range(QUAD):
                            last_mm = flip128(nc, p_t[:, j * P:(j + 1) * P], rows[h][:, j, :],
                                                          K["ident"][:, :])
                        last_mm.then_inc(s_pt, 1)
                        pe.wait_ge(s_ht, q + 1)
                        pe.wait_ge(s_ew[h], 16 * (i + 1))
                        if not (first and h == 0):
                            pe.wait_ge(s_e1, q)
                        nc.tensor.matmul(p_1[:, :], weights["W1"][:, :], ht[:, :], start=True, stop=False)
                        nc.tensor.matmul(p_1[:, :], weights["w1d"][:, :], ew[h][:, :], start=False,
                                         stop=True).then_inc(s_p1, 1)
                        pe.wait_ge(s_e1, q + 1)
                        if not (first and h == 0):
                            pe.wait_ge(s_e2, q)
                        for j in range(QUAD):
                            nc.tensor.matmul(p_2[:, j, :], e1[:, j * P:(j + 1) * P], weights["W2"][:, :],
                                             start=True, stop=False)
                            last_mm = nc.tensor.matmul(p_2[:, j, :], K["ones"][0:1, :],
                                                       weights["b2"][0:1, :], start=False, stop=True)
                        last_mm.then_inc(s_p2, 1)
                        pe.wait_ge(s_e2, q + 1)
                    pe.wait_ge(s_same, q + 1)
                    if not first:
                        pe.wait_ge(s_total, q - 1)
                    if kind == "rel":
                        def finish(j):
                            pe.wait_ge(s_ztb, 4 * q + j + 1)
                            for c in range(4):
                                mm = nc.tensor.matmul(p_sum[h][:, j, 0:D], ztb[j % 2][:, c, :],
                                                      weights["W"][:, c, :], start=c == 0, stop=c == 3)
                            return mm
                        for j in range(QUAD):
                            pe.wait_ge(s_z, 4 * q + j + 1)
                            if not (first and h == 0 and j < 2):
                                pe.wait_ge(s_ztb, 4 * q + j - 1)
                            for c in range(4):
                                mm = nc.tensor.matmul(
                                    p_zt[j % 2][:, c, :],
                                    z[j % 2][:, 2 * c:2 * c + 2, :].rearrange("p r f -> p (r f)"),
                                    same[h][:, j, :], start=True, stop=True)
                            mm.then_inc(s_zt, 1)
                            if j:
                                finish(j - 1)
                        finish(QUAD - 1).then_inc(s_sum, 1)
                    else:
                        message = e2 if kind == "mlp" else rows[h]
                        for j in range(QUAD):
                            mm = nc.tensor.matmul(p_sum[h][:, j, 0:width], same[h][:, j, :],
                                                  message[:, j, :], start=True, stop=True)
                        mm.then_inc(s_sum, 1)

            rounds(pe, ROUNDS, body)

        @block.scalar
        def _(act):
            def body(i, first, last):
                for h in range(2):
                    q = i * 2 + h
                    if kind == "rel":
                        for j in range(QUAD):
                            act.wait_ge(s_zt, 4 * q + j + 1)
                            nc.scalar.copy(ztb[j % 2][:, :, :], p_zt[j % 2][:, :, :]).then_inc(s_ztb, 1)
                    if kind == "mlp":
                        act.wait_ge(s_pt, q + 1)
                        if not (first and h == 0):
                            act.wait_ge(s_p1, q)
                        nc.scalar.copy(ht[:, :], p_t[:, :]).then_inc(s_ht, 1)
                        act.wait_ge(s_p1, q + 1)
                        if not (first and h == 0):
                            act.wait_ge(s_p2, q)
                        nc.scalar.activation(e1[:, :], p_1[:, :], ACT.Silu,
                                             bias=weights["b1"][:, 0:1]).then_inc(s_e1, 1)
                        act.wait_ge(s_p2, q + 1)
                        if not (first and h == 0):
                            act.wait_ge(s_sum, q)
                        nc.scalar.activation(e2[:, :, :], p_2[:, :, :], ACT.Silu).then_inc(s_e2, 1)
                    else:
                        act.wait_ge(s_sum, q + 1)
                        if not first:
                            scattered(act, q)
                        nc.scalar.copy(total[h][:, :, :], p_sum[h][:, :, 0:width]).then_inc(s_total, 1)

            rounds(act, ROUNDS, body)

        inner.close()
        clear(nc, sems)


def prepare(nc, K, src, dst, rel, x, xp):
    with ExitStack() as ctx:
        def sb(name, shape, dt=F32):
            return ctx.enter_context(nc.sbuf_tensor(f"pre_{name}", shape, dt))

        sems = []

        def sem(name):
            sems.append(ctx.enter_context(nc.semaphore(f"pre_{name}")))
            return sems[-1]

        lists = (("src", src, PADKEY), ("dst", dst, PADKEY), ("rel", rel, 0))
        raw = [sb(f"raw_{n}", [QUADS, QE], I32) for n, _, _ in lists]
        rawf = [sb(f"rawf_{n}", [QUADS, QE]) for n, _, _ in lists]
        high = [sb(f"high{k}", [P, QUAD, QUADS]) for k in range(2)]
        low = [sb(f"low{k}", [P, QUAD, QUADS]) for k in range(2)]
        highi = sb("highi", [P, QUAD, QUADS], I32)
        below = sb("below", [P, QUAD, QUADS])
        iotai = sb("iotai", [P, T], I32)
        iota16 = sb("iota16", [P, T], F16)
        sparei = sb("sparei", [P, 1], I32)
        hot_high = [[sb(f"hot_high{k}{h}", [P, QUAD, P], F16) for h in range(2)] for k in range(2)]
        hot_low = [[sb(f"hot_low{k}{h}", [P, QUAD, T], F16) for h in range(2)] for k in range(2)]
        root = sb("root", [P, T])
        present = sb("present", [P, T])
        p_t = [ctx.enter_context(nc.psum_tensor(f"pre_p_t{k}", [P, QUAD, P], F32)) for k in range(3)]
        p_deg = [ctx.enter_context(nc.psum_tensor(f"pre_p_deg{k}", [P, 512], F32)) for k in range(2)]

        s_padded = sem("padded")
        s_raw = sem("raw")
        s_x = sem("x")
        s_zero = sem("zero")
        s_const = sem("const")
        s_rawf = sem("rawf")
        s_pt = sem("pt")
        s_v = sem("v")
        s_hot = sem("hot")
        s_deg = sem("deg")
        s_max = sem("max")
        s_root = sem("root")
        inner = ctx.enter_context(ExitStack())
        block = inner.enter_context(nc.Block())

        @block.gpsimd
        def _(pool):
            nc.gpsimd.memset(K["ident"][:, :], 0.0).then_inc(s_const, 1)
            nc.gpsimd.memset(K["before"][:, :], 1.0).then_inc(s_const, 1)
            pool.wait_ge(s_const, 2)
            nc.gpsimd.affine_select(out=K["ident"][:, :], in_=K["ident"][:, :],
                                    compare_op=ALU.not_equal, fill=1.0, base=0, pattern=[[-1, P]],
                                    channel_multiplier=1).then_inc(s_const, 1)
            nc.gpsimd.affine_select(out=K["before"][:, :], in_=K["before"][:, :],
                                    compare_op=ALU.is_gt, fill=0.0, base=0, pattern=[[-1, P]],
                                    channel_multiplier=1).then_inc(s_const, 1)
            nc.gpsimd.iota(iotai[:, :], [[1, T]], base=0, channel_multiplier=0).then_inc(s_const, 1)
            nc.gpsimd.iota(sparei[:, :], [[1, 1]], base=NR, channel_multiplier=1).then_inc(s_const, 1)

        @block.sync
        def _(sp):
            sp.wait_ge(s_padded, 3)
            for n, (_, a, _) in enumerate(lists):
                sp.dma_start(raw[n][0:96, :], a[0:96 * QE].rearrange("(q e) -> q e", e=QE)).then_inc(s_raw, 16)
                sp.dma_start(raw[n][96:97, :], a[96 * QE:97 * QE].rearrange("(q e) -> q e", e=QE)).then_inc(s_raw, 16)
                sp.dma_start(raw[n][97:98, 0:RESTQ], a[97 * QE:N].rearrange("(q e) -> q e", q=1)).then_inc(s_raw, 16)
            sp.dma_start(xp[0:N, :].rearrange("(a n) f -> a (n f)", a=16),
                         x.rearrange("(a n) f -> a (n f)", a=16)).then_inc(s_x, 16)
            sp.wait_ge(s_zero, 1)
            sp.dma_start(xp[N:NR, :].rearrange("(a n) f -> a (n f)", a=16),
                         K["zero"][0:16, 0:(NR - N) // 16 * D]).then_inc(s_x, 16)
            sp.wait_ge(s_x, 32)

        @block.vector
        def _(dve):
            for n, (_, _, pad) in enumerate(lists):
                nc.vector.memset(raw[n][:, :], pad).then_inc(s_padded, 1)
            nc.vector.memset(K["zero"][:, :], 0.0).then_inc(s_zero, 1)
            nc.vector.memset(K["ones"][:, :], 1.0)
            nc.vector.memset(K["eps"][:, :], EPS)
            dve.wait_ge(s_raw, 16 * 9)
            for n in range(3):
                nc.vector.tensor_copy(rawf[n][:, :], raw[n][:, :]).then_inc(s_rawf, 1)
            dve.wait_ge(s_const, 6)
            nc.vector.tensor_copy(K["iota"][:, :], iotai[:, :])
            nc.vector.tensor_copy(iota16[:, :], iotai[:, :])
            nc.vector.tensor_copy(K["spare"][:, :], sparei[:, :])
            v = 0
            for n, name in enumerate(("src", "dst", "rel")):
                dve.wait_ge(s_pt, n + 1)
                nc.vector.tensor_copy(K[name][:, :, :], p_t[n][:, :, 0:QUADS]).then_inc(s_v, 1)
                v += 1
                if n < 2:
                    nc.vector.tensor_copy(K[name + "i"][:, :, :], p_t[n][:, :, 0:QUADS]).then_inc(s_v, 1)
                    v += 1
                    dve.wait_ge(s_v, v)
                    nc.vector.tensor_scalar(highi[:, :, :], K[name][:, :, :], 1.0 / T, 0.5 / T,
                                            ALU.mult, ALU.add).then_inc(s_v, 1)
                    dve.wait_ge(s_v, v + 1)
                    nc.vector.tensor_copy(high[n][:, :, :], highi[:, :, :]).then_inc(s_v, 1)
                    dve.wait_ge(s_v, v + 2)
                    nc.vector.scalar_tensor_tensor(out=low[n][:, :, :], in0=high[n][:, :, :],
                                                   scalar=float(-T), in1=K[name][:, :, :],
                                                   op0=ALU.mult, op1=ALU.add).then_inc(s_v, 1)
                    dve.wait_ge(s_v, v + 3)
                    nc.vector.tensor_scalar(below[:, :, :], low[n][:, :, :], 0.0, None, ALU.is_lt
                                            ).then_inc(s_v, 1)
                    dve.wait_ge(s_v, v + 4)
                    nc.vector.tensor_tensor(high[n][:, :, :], high[n][:, :, :], below[:, :, :],
                                            ALU.subtract).then_inc(s_v, 1)
                    nc.vector.scalar_tensor_tensor(out=low[n][:, :, :], in0=below[:, :, :],
                                                   scalar=float(T), in1=low[n][:, :, :],
                                                   op0=ALU.mult, op1=ALU.add).then_inc(s_v, 1)
                    v += 6
            dve.wait_ge(s_v, v)

            def body(i, first, last):
                for h in range(2):
                    q = i * 2 + h
                    if not first:
                        dve.wait_ge(s_deg, q - 1)
                    for k in range(2):
                        for j in range(QUAD):
                            nc.vector.tensor_scalar(hot_high[k][h][:, j, :], iota16[:, 0:P],
                                                    high[k][:, j, bass.ds(q, 1)], None, ALU.is_equal)
                            op = nc.vector.tensor_scalar(hot_low[k][h][:, j, :], iota16[:, :],
                                                         low[k][:, j, bass.ds(q, 1)], None, ALU.is_equal)
                    op.then_inc(s_hot, 1)

            rounds(dve, ROUNDS, body)
            dve.wait_ge(s_deg, QUADS)
            nc.vector.tensor_scalar(present[:, :], p_deg[0][:, 0:T], 0.5, None, ALU.is_gt).then_inc(s_v, 1)
            nc.vector.tensor_scalar(K["dis"][:, :], p_deg[0][:, 0:T], 1.0, None, ALU.max).then_inc(s_max, 1)
            nc.vector.tensor_scalar(K["dinv"][:, :], p_deg[1][:, 0:T], 1.0, None, ALU.add).then_inc(s_max, 1)
            for k, name in enumerate(("dis", "dinv")):
                dve.wait_ge(s_root, k + 1)
                nc.vector.reciprocal(K[name][:, :], K[name][:, :]).then_inc(s_v, 1)
            dve.wait_ge(s_v, v + 3)
            nc.vector.tensor_tensor(K["dis"][:, :], K["dis"][:, :], present[:, :], ALU.mult)

        @block.tensor
        def _(pe):
            pe.wait_ge(s_const, 6)
            for n in range(3):
                pe.wait_ge(s_rawf, n + 1)
                for j in range(QUAD):
                    mm = flip128(nc, p_t[n][:, j, 0:QUADS], rawf[n][:, j * P:(j + 1) * P],
                                             K["ident"][0:QUADS, 0:QUADS])
                mm.then_inc(s_pt, 1)

            def body(i, first, last):
                for h in range(2):
                    q = i * 2 + h
                    pe.wait_ge(s_hot, q + 1)
                    for j in range(QUAD):
                        for k in range(2):
                            mm = nc.tensor.matmul(p_deg[k][:, 0:T], hot_high[k][h][:, j, :],
                                                  hot_low[k][h][:, j, :],
                                                  start=first and h == 0 and j == 0,
                                                  stop=last and h == 1 and j == QUAD - 1)
                    mm.then_inc(s_deg, 1)

            rounds(pe, ROUNDS, body)

        @block.scalar
        def _(act):
            for k, name in enumerate(("dis", "dinv")):
                act.wait_ge(s_max, k + 1)
                nc.scalar.activation(K[name][:, :], K[name][:, :], ACT.Sqrt).then_inc(s_root, 1)

        inner.close()
        clear(nc, sems)


def node_pass(nc, label, K, kind, ins, outs, zero=None, weights=None):
    matmuls = kind in ("mlp", "conv1", "conv2")
    normed = kind in ("norm0", "norm", "mlp", "conv2")
    with ExitStack() as ctx:
        def sb(name, shape, dt=F32):
            return ctx.enter_context(nc.sbuf_tensor(f"{label}_{name}", shape, dt))

        def ps(name, shape):
            return ctx.enter_context(nc.psum_tensor(f"{label}_{name}", shape, F32))

        sems = []

        def sem(name):
            sems.append(K["semaphore"](f"node_{name}"))
            return sems[-1]

        widths = [t.shape[1] for t in ins]
        got = [[sb(f"in{n}_{h}", [P, CH, w]) for h in range(2)] for n, w in enumerate(widths)]
        result = [[sb(f"out{n}_{h}", [P, CH, D]) for h in range(2)] for n in range(len(outs))]
        s_in = [sem(f"in{h}") for h in range(2)]
        s_out = [sem(f"out{h}") for h in range(2)]
        s_done = sem("done")
        s_v = sem("v")
        s_zero = sem("zero")
        s_turn = sem("turn")
        s_c = sem("c")
        s_sq = sem("sq")
        s_var = sem("var")
        s_std = sem("std")
        s_x3 = sem("x3")
        sumv = sb("sumv", [P, CH, D])
        cent = sb("cent", [P, CH, D])
        sq = sb("sq", [P, CH, D])
        mean = sb("mean", [P, CH])
        var = sb("var", [P, CH])
        std = sb("std", [P, CH])
        rstd = sb("rstd", [P, CH])
        if matmuls:
            NQ = CH // QUAD
            s_z = sem("z")
            s_pt = sem("pt")
            s_t = sem("t")
            s_p = sem("p")
            s_u = sem("u")
            s_p2 = sem("p2")
            s_got = sem("got")
            s_last = s_p2 if kind == "mlp" else s_p
            hid = sb("hid", [P, CH, D])
            tin = [sb(f"tin{h}", [P, QE]) for h in range(2)]
            txin = [sb(f"txin{h}", [P, QE]) for h in range(2)]
            u = [sb(f"u{h}", [P, QE]) for h in range(2)]
            both = sb("both", [P, CH, 2 * D])
            p_t = [ps(f"p_t{h}", [P, QE]) for h in range(2)]
            p_tx = [ps(f"p_tx{h}", [P, QE]) for h in range(2)]
            p_1 = [ps(f"p_1{h}", [P, QE]) for h in range(2)] if kind == "mlp" else None
            p_o = [ps(f"p_o{h}", [P, QUAD, P]) for h in range(2)]
        inner = ctx.enter_context(ExitStack())
        block = inner.enter_context(nc.Block())

        @block.sync
        def _(sp):
            def load(c, h):
                for n, table in enumerate(ins):
                    w = widths[n]
                    sp.dma_start(got[n][h][:, :, :].rearrange("p t f -> p (t f)"),
                                 table[0:NR, :].rearrange("(p t) f -> p (t f)", p=P)[:, bass.ds(c * (CH * w), CH * w)]
                                 ).then_inc(s_in[h], 16)

            load(0, 0)

            def body(i, first, last):
                for h in range(2):
                    c = i * 2 + h
                    if not (last and h == 1):
                        if not (first and h == 0):
                            sp.wait_ge(s_done, c)
                        load(c + 1, 1 - h)
                    sp.wait_ge(s_done, c + 1)
                    for n, table in enumerate(outs):
                        value = result[n][h][:, :, :].rearrange("p t f -> p (t f)")
                        if kind != "conv2":
                            sp.dma_start(chunk_of(table, c), value).then_inc(s_out[h], 16)
                        else:
                            full, tail = table
                            rows_of = full[0:LASTP * T, :].rearrange("(p t) f -> p (t f)", p=LASTP)
                            sp.dma_start(rows_of[0:112, bass.ds(c * CW, CW)], value[0:112, :]).then_inc(s_out[h], 16)
                            sp.dma_start(rows_of[112:LASTP, bass.ds(c * CW, CW)], value[112:LASTP, :]).then_inc(s_out[h], 16)
                            sp.dma_start(tail.rearrange("(a t) f -> a (t f)", a=1)[:, bass.ds(c * CW, CW)],
                                         value[LASTP:P, :]).then_inc(s_out[h], 16)

            rounds(sp, CROUNDS, body)
            each = 3 if kind == "conv2" else len(outs)
            for h in range(2):
                sp.wait_ge(s_out[h], 16 * each * CROUNDS)
            if kind == "conv2":
                full, tail = outs[0]
                sp.dma_start(full[LASTP * T:N, :].rearrange("(a n) f -> a (n f)", a=8),
                             tail[0:LASTT, :].rearrange("(a n) f -> a (n f)", a=8)).then_inc(s_zero, 16)
                sp.wait_ge(s_zero, 16)

        stores = 3 if kind == "conv2" else len(outs)

        @block.vector
        def _(dve):
            if matmuls and kind != "conv2":
                for h in range(2):
                    nc.vector.memset(txin[h][D:D + 1, :], 1.0).then_inc(s_z, 1)
            def count_steps():
                n = {"scale": 1, "norm0": 3, "norm": 2, "mlp": 0, "conv1": 2, "conv2": 3}[kind]
                return n + (3 if normed else 0)
            per = count_steps()

            def body(i, first, last):
                for h in range(2):
                    c = i * 2 + h
                    k = [0]

                    def own(op):
                        k[0] += 1
                        op.then_inc(s_v, 1)
                        dve.wait_ge(s_v, c * per + k[0])

                    dve.wait_ge(s_in[h], 16 * len(ins) * (i + 1))
                    if not first:
                        dve.wait_ge(s_out[h], 16 * stores * i)
                    dis = bc(K["dis"][:, bass.ds(c * CH, CH)].unsqueeze(2), [P, CH, D])
                    dinv = bc(K["dinv"][:, bass.ds(c * CH, CH)].unsqueeze(2), [P, CH, D])
                    g = [got[n][h][:, :, :] for n in range(len(ins))]
                    if kind == "scale":
                        nc.vector.tensor_tensor(result[0][h][:, :, :], g[0], dis, ALU.mult).then_inc(s_done, 1)
                        continue
                    if kind == "norm0":
                        own(nc.vector.tensor_tensor(sumv[:, :, :], g[1], g[2], ALU.add))
                        own(nc.vector.tensor_tensor(sumv[:, :, :], sumv[:, :, :], dis, ALU.mult))
                        own(nc.vector.tensor_tensor(sumv[:, :, :], sumv[:, :, :], g[0], ALU.add))
                    if kind == "norm":
                        own(nc.vector.tensor_tensor(sumv[:, :, :], g[1], g[2], ALU.add))
                        own(nc.vector.tensor_tensor(sumv[:, :, :], sumv[:, :, :], g[0], ALU.add))
                    if kind in ("conv1", "conv2"):
                        z = both[:, :, 0:D]
                        if not (first and h == 0):
                            dve.wait_ge(s_pt, c * NQ)
                        if kind == "conv2":
                            own(nc.vector.tensor_copy(both[:, :, D:2 * D], g[3]))
                        own(nc.vector.tensor_tensor(z, g[0], g[1], ALU.add))
                        own(nc.vector.tensor_tensor(z, z, g[2], ALU.add))
                        nc.vector.tensor_tensor(z, z, dinv, ALU.mult).then_inc(s_z, 1)
                    if kind == "conv1":
                        dve.wait_ge(s_got, (c + 1) * NQ)
                        nc.vector.tensor_tensor(result[0][h][:, :, :], hid[:, :, :], dinv, ALU.mult).then_inc(s_done, 1)
                        continue
                    if kind in ("mlp", "conv2"):
                        kept = g[0] if kind == "mlp" else g[3]
                        for n in range(NQ):
                            dve.wait_ge(s_last, c * NQ + n + 1)
                            nc.vector.tensor_tensor(sumv[:, n * QUAD:(n + 1) * QUAD, :],
                                                    p_o[n % 2][:, :, 0:D], kept[:, n * QUAD:(n + 1) * QUAD, :],
                                                    ALU.add).then_inc(s_got, 1)
                        dve.wait_ge(s_got, (c + 1) * NQ)
                    own(nc.vector.tensor_reduce(mean[:, :], sumv[:, :, :], AX.X, ALU.add))
                    own(nc.vector.tensor_scalar(mean[:, :], mean[:, :], 1.0 / D, None, ALU.mult))
                    nc.vector.tensor_tensor(cent[:, :, :], sumv[:, :, :],
                                            bc(mean[:, :].unsqueeze(2), [P, CH, D]), ALU.subtract).then_inc(s_c, 1)
                    dve.wait_ge(s_sq, c + 1)
                    nc.vector.tensor_reduce(var[:, :], sq[:, :, :], AX.X, ALU.add).then_inc(s_var, 1)
                    dve.wait_ge(s_std, c + 1)
                    own(nc.vector.reciprocal(rstd[:, :], std[:, :]))
                    op = nc.vector.tensor_tensor(result[0][h][:, :, :], cent[:, :, :],
                                                 bc(rstd[:, :].unsqueeze(2), [P, CH, D]), ALU.mult)
                    if kind == "mlp":
                        op.then_inc(s_x3, 1)
                        dve.wait_ge(s_x3, c + 1)
                        op = nc.vector.tensor_tensor(result[1][h][:, :, :], result[0][h][:, :, :], dinv, ALU.mult)
                    op.then_inc(s_done, 1)

            rounds(dve, CROUNDS, body)

        @block.scalar
        def _(act):
            def body(i, first, last):
                for h in range(2):
                    c = i * 2 + h
                    if matmuls:
                        if kind == "conv1" and not (first and h == 0):
                            act.wait_ge(s_done, c)
                        for n in range(NQ):
                            m = c * NQ + n
                            b = n % 2
                            act.wait_ge(s_pt, m + 1)
                            if not (first and h == 0 and n < 2):
                                act.wait_ge(s_p, m - 1)
                            if kind == "mlp":
                                nc.scalar.copy(txin[b][0:D, :], p_tx[b][0:D, :])
                                nc.scalar.copy(tin[b][:, :], p_t[b][:, :]).then_inc(s_t, 1)
                                act.wait_ge(s_p, m + 1)
                                if not (first and h == 0 and n < 2):
                                    act.wait_ge(s_p2, m - 1)
                                nc.scalar.activation(u[b][:, :], p_1[b][:, :], ACT.Silu,
                                                     bias=weights["b1"][:, 0:1]).then_inc(s_u, 1)
                            elif kind == "conv1":
                                nc.scalar.copy(txin[b][0:D, :], p_tx[b][0:D, :]).then_inc(s_t, 1)
                                act.wait_ge(s_p, m + 1)
                                nc.scalar.activation(hid[:, n * QUAD:(n + 1) * QUAD, :],
                                                     p_o[b][:, :, 0:D], ACT.Relu).then_inc(s_got, 1)
                            else:
                                nc.scalar.copy(tin[b][:, :], p_t[b][:, :]).then_inc(s_t, 1)
                    if normed:
                        act.wait_ge(s_c, c + 1)
                        nc.scalar.activation(sq[:, :, :], cent[:, :, :], ACT.Square).then_inc(s_sq, 1)
                        act.wait_ge(s_var, c + 1)
                        nc.scalar.activation(std[:, :], var[:, :], ACT.Sqrt, scale=1.0 / D,
                                             bias=K["eps"][:, 0:1]).then_inc(s_std, 1)

            if kind != "scale":
                rounds(act, CROUNDS, body)

        @block.tensor
        def _(pe):
            if not matmuls:
                return
            zb = 0 if kind == "conv2" else 2
            if kind == "mlp":
                pe.wait_ge(s_z, 2)

            def body(i, first, last):
                for h in range(2):
                    c = i * 2 + h

                    def flip(n):
                        b = n % 2
                        if not (first and h == 0 and n < 2):
                            pe.wait_ge(s_t, c * NQ + n - 1)
                        for j in range(QUAD):
                            t = n * QUAD + j
                            if kind == "mlp":
                                flip128(nc, p_t[b][:, j * P:(j + 1) * P], got[1][h][:, t, :], K["ident"][:, :])
                                mm = flip128(nc, p_tx[b][0:D, j * P:(j + 1) * P], got[0][h][:, t, :], K["ident"][:, :])
                            elif kind == "conv1":
                                if j == 0:
                                    pe.sem_inc(s_turn, 1)
                                mm = flip128(nc, p_tx[b][0:D, j * P:(j + 1) * P], both[:, t, 0:D], K["ident"][:, :])
                            else:
                                mm = flip128(nc, p_t[b][:, j * P:(j + 1) * P], both[:, t, :], K["ident"][:, :])
                        mm.then_inc(s_pt, 1)

                    pe.wait_ge(s_in[h], 16 * len(ins) * (i + 1))
                    if kind != "mlp":
                        pe.wait_ge(s_z, c + 1 + zb)
                    flip(0)
                    for n in range(NQ):
                        m = c * NQ + n
                        b = n % 2
                        if n + 1 < NQ:
                            flip(n + 1)
                        pe.wait_ge(s_t, m + 1)
                        if kind == "mlp":
                            if not (first and h == 0 and n < 2):
                                pe.wait_ge(s_u, m - 1)
                            nc.tensor.matmul(p_1[b][:, :], weights["Wx"][:, :], txin[b][0:D, :], start=True, stop=False)
                            nc.tensor.matmul(p_1[b][:, :], weights["Wa"][:, :], tin[b][:, :], start=False, stop=True).then_inc(s_p, 1)
                            pe.wait_ge(s_u, m + 1)
                            if not (first and h == 0 and n < 2):
                                pe.wait_ge(s_got, m - 1)
                            for j in range(QUAD):
                                nc.tensor.matmul(p_o[b][:, j, 0:D], u[b][:, j * P:(j + 1) * P], weights["W2"][:, :], start=True, stop=False)
                                mm = nc.tensor.matmul(p_o[b][:, j, 0:D], K["ones"][0:1, :], weights["b2"][0:1, :], start=False, stop=True)
                            mm.then_inc(s_p2, 1)
                        else:
                            if not (first and h == 0 and n < 2):
                                pe.wait_ge(s_got, m - 1)
                            for j in range(QUAD):
                                if kind == "conv1":
                                    mm = nc.tensor.matmul(p_o[b][:, j, 0:D], txin[b][0:D + 1, j * P:(j + 1) * P],
                                                          weights["W1b"][0:D + 1, :], start=True, stop=True)
                                else:
                                    nc.tensor.matmul(p_o[b][:, j, 0:D], tin[b][:, j * P:(j + 1) * P], weights["W2e"][:, :], start=True, stop=False)
                                    mm = nc.tensor.matmul(p_o[b][:, j, 0:D], K["ones"][0:2, :], weights["b2e"][0:2, :], start=False, stop=True)
                            mm.then_inc(s_p, 1)

            rounds(pe, CROUNDS, body)

        inner.close()
        clear(nc, sems)


def gnn(nc, x, src, dst, rel, ew, W, eW1, eb1, eW2, eb2, nW1, nb1, nW2, nb2, W1, b1, W2, b2, We, be, out):
    def table(name, rows=NR, width=D):
        return nc.dram_tensor(name, [rows, width], F32, kind="Internal").ap()

    xp = table("x_padded")
    y0 = table("y0")
    x1 = table("x1")
    x2 = table("x2")
    x3 = table("x3")
    y3 = table("y3")
    y4 = table("y4")
    tail = table("out_tail", T)
    sums0 = [table(f"sums0_{n}", NA) for n in range(2)]
    sums1 = [table(f"sums1_{n}", NA) for n in range(2)]
    sums2 = [table("sums2", NA, HID)]
    sums3 = [table(f"sums3_{n}", NA) for n in range(2)]
    sums4 = [table(f"sums4_{n}", NA) for n in range(2)]
    with ExitStack() as ctx:
        def sb(name, shape, dt=F32):
            return ctx.enter_context(nc.sbuf_tensor(name, shape, dt))

        K = {name: sb(name, shape) for name, shape in (
            ("ident", [P, P]), ("before", [P, P]), ("iota", [P, T]), ("spare", [P, 1]), ("eps", [P, 1]),
            ("ones", [2, P]), ("src", [P, QUAD, QUADS]), ("dst", [P, QUAD, QUADS]),
            ("rel", [P, QUAD, QUADS]), ("dis", [P, T]), ("dinv", [P, T]), ("zero", [P, 3144]))}
        semaphores = {}

        def semaphore(name):
            if name not in semaphores:
                semaphores[name] = ctx.enter_context(nc.semaphore(name))
            return semaphores[name]

        K["semaphore"] = semaphore
        K["srci"] = sb("srci", [P, QUAD, QUADS], I32)
        K["dsti"] = sb("dsti", [P, QUAD, QUADS], I32)
        wrel = sb("wrel", [P, 4, D])
        we1 = sb("we1", [P, HID])
        we1d = sb("we1d", [1, HID])
        we2 = sb("we2", [P, HID])
        be1 = sb("be1", [P, 1])
        be2 = sb("be2", [1, HID])
        wnx = sb("wnx", [D, HID])
        wna = sb("wna", [HID, HID])
        wn2 = sb("wn2", [HID, D])
        bn1 = sb("bn1", [P, 1])
        bn2 = sb("bn2", [1, D])
        w1b = sb("w1b", [D + 1, D])
        w2e = sb("w2e", [2 * D, D])
        b2e = sb("b2e", [2, D])

        def row(a):
            return a.rearrange("(a n) -> a n", a=1)

        def column(a):
            return a.rearrange("(n a) -> n a", a=1)

        loads = ((wrel[:, :, :], W.rearrange("(c r) i h -> (r i) c h", r=2)), (we1[:, :], eW1[0:2 * D, :]),
                 (we1d[:, :], eW1[2 * D:2 * D + 1, :]), (we2[:, :], eW2), (be1[:, :], column(eb1)),
                 (be2[:, :], row(eb2)), (wnx[:, :], nW1[0:D, :]), (wna[:, :], nW1[D:D + HID, :]),
                 (wn2[:, :], nW2), (bn1[:, :], column(nb1)), (bn2[:, :], row(nb2)),
                 (w1b[0:D, :], W1), (w1b[D:D + 1, :], row(b1)), (w2e[0:D, :], W2), (w2e[D:2 * D, :], We),
                 (b2e[0:1, :], row(b2)), (b2e[1:2, :], row(be)))
        s_weights = ctx.enter_context(nc.semaphore("s_weights"))
        s_clear = ctx.enter_context(nc.semaphore("s_clear"))
        with nc.Block() as block:
            @block.sync
            def _(sp):
                for to, of in loads:
                    sp.dma_start(to, of).then_inc(s_weights, 16)
                sp.wait_ge(s_weights, 16 * len(loads))

        prepare(nc, K, src, dst, rel, x, xp)
        with nc.Block() as block:
            @block.sync
            def _(sp):
                for t in sums0:
                    flat = t.rearrange("(p t) f -> p (t f)", p=P)
                    for a in range(0, flat.shape[1], 3144):
                        sp.dma_start(flat[:, a:a + 3144], K["zero"][:, :]).then_inc(s_clear, 16)
                sp.wait_ge(s_clear, 16 * 2 * 8)

        node_pass(nc, "n0", K, "scale", [xp], [y0])
        edge_pass(nc, "e0", K, [(y0, K["dsti"])], K["src"], sums0, D, "plain", zero=(K["zero"], sums1, 3144))
        node_pass(nc, "n1", K, "norm0", [xp] + sums0, [x1])
        edge_pass(nc, "e1", K, [(x1, K["srci"])], K["dst"], sums1, D, "rel", zero=(K["zero"], sums2, 3144),
                  weights={"W": wrel})
        node_pass(nc, "n2", K, "norm", [x1] + sums1, [x2])
        edge_pass(nc, "e2", K, [(x2, K["srci"]), (x2, K["dsti"])], K["src"], sums2, HID, "mlp",
                  zero=(K["zero"], sums3, 3144),
                  weights={"W1": we1, "w1d": we1d, "W2": we2, "b1": be1, "b2": be2, "ew": ew})
        node_pass(nc, "n3", K, "mlp", [x2] + sums2, [x3, y3],
                  weights={"Wx": wnx, "Wa": wna, "W2": wn2, "b1": bn1, "b2": bn2})
        edge_pass(nc, "e3", K, [(y3, K["srci"])], K["dst"], sums3, D, "plain", zero=(K["zero"], sums4, 3144))
        node_pass(nc, "n4", K, "conv1", sums3 + [y3], [y4], weights={"W1b": w1b})
        edge_pass(nc, "e4", K, [(y4, K["srci"])], K["dst"], sums4, D, "plain")
        node_pass(nc, "n5", K, "conv2", sums4 + [y4, x3], [(out, tail)], weights={"W2e": w2e, "b2e": b2e})


_INS = ["x", "src", "dst", "edge_type_8", "edge_weight1", "L1_gnn_W", "L2_gnn_eW1", "L2_gnn_eb1",
        "L2_gnn_eW2", "L2_gnn_eb2", "L2_gnn_nW1", "L2_gnn_nb1", "L2_gnn_nW2", "L2_gnn_nb2",
        "L3_gnn_W1", "L3_gnn_b1", "L3_gnn_W2", "L3_gnn_b2", "L3_gnn_W_emb", "L3_gnn_b_emb"]


def kernel(**inputs):
    import numpy as _np
    import concourse.bacc as _bacc
    from concourse import mybir as _mybir
    from concourse.bass_utils import run_bass_kernel_spmd as _run

    nc = _bacc.Bacc("TRN2", target_bir_lowering=False, num_devices=1)
    arrays, args = {}, []
    for name in _INS:
        a = _np.ascontiguousarray(inputs[name])
        if name == "edge_weight1":
            a = a.reshape(-1)
        arrays[f"in_{name}"] = a
        args.append(nc.dram_tensor(f"in_{name}", a.shape, _mybir.dt.from_np(a.dtype), kind="ExternalInput").ap())
    args.append(nc.dram_tensor("out_x", (N, D), F32, kind="ExternalOutput").ap())
    gnn(nc, *args)
    r = _run(nc, [arrays], core_ids=[0])
    return r.results[0]["out_x"]
```

```python
import numpy as np
import concourse.bass as bass
from concourse import mybir
from contextlib import ExitStack

F32 = mybir.dt.float32
F16 = mybir.dt.float16
I32 = mybir.dt.int32
ALU = mybir.AluOpType
ACT = mybir.ActivationFunctionType
AX = mybir.AxisListType

P = 128
N = 50000
D = 64
HID = 128
REL = 8
QUAD = 4
QUADS = 98
ROUNDS = QUADS // 2
QE = QUAD * P
FULLQ = N // QE
RESTQ = N - FULLQ * QE
T = QUADS * QUAD
NR = P * T
PADKEY = NR - 1
NA = NR + P
CH = 28
CHUNKS = T // CH
CROUNDS = CHUNKS // 2
CW = CH * D
LASTP = P - 1
LASTT = N - LASTP * T
EPS = 1e-5
XPARTS = 8
XC = T // XPARTS
XW = XC * D
PIECE = NA * D // P // 8


def bc(ap, shape):
    return ap.to_broadcast(shape)


def flip128(nc, out, a, ident):
    return nc.tensor.matmul(out, a, ident, is_transpose=True, start=True, stop=True)


def clear(nc, sems):
    with nc.Block() as block:
        @block.gpsimd
        def _(pool):
            for s in sems:
                pool.sem_clear(s)


def rounds(eng, count, body):
    body(0, True, False)
    with eng.Fori(1, count - 1) as i:
        body(i, False, False)
    body(count - 1, False, True)


def chunk_of(table, c):
    return table[0:NR, :].rearrange("(p t) f -> p (t f)", p=P)[:, bass.ds(c * CW, CW)]


def one_hot(nc, K, high, low, columns, hot_high, hot_low):
    for j in range(QUAD):
        nc.vector.tensor_scalar(hot_high[:, j, :], K["iota16"][:, 0:P], high[:, j, columns], None, ALU.is_equal)
        op = nc.vector.tensor_scalar(hot_low[:, j, :], K["iota16"][:, :], low[:, j, columns], None, ALU.is_equal)
    return op


def edge_pass(nc, label, K, sources, key, sums, width, kind, zero=(), weights=None, degrees=False):
    ng = len(sources)
    nt = len(sums)
    with ExitStack() as ctx:
        def sb(name, shape, dt=F32):
            return ctx.enter_context(nc.sbuf_tensor(f"{label}_{name}", shape, dt))

        def ps(name, shape):
            return ctx.enter_context(nc.psum_tensor(f"{label}_{name}", shape, F32))

        sems = []

        def sem(name):
            sems.append(K["semaphore"](f"edge_{name}"))
            return sems[-1]

        def own_sem(name):
            return K["semaphore"](f"{label}_{name}")

        gidx = [[sb(f"gidx{g}_{h}", [P, QUAD], I32) for h in range(2)] for g in range(ng)]
        rows = [sb(f"rows{h}", [P, QUAD, D * ng]) for h in range(2)]
        keys = [sb(f"keys{h}", [P, QUAD]) for h in range(2)]
        same = [sb(f"same{h}", [P, QUAD, P]) for h in range(2)]
        sidx = [sb(f"sidx{h}", [P, QUAD], I32) for h in range(2)]
        total = [sb(f"total{h}", [P, QUAD, width]) for h in range(2)]
        earlier = sb("earlier", [P, QUAD])
        scratch = sb("scratch", [P, P])
        away = sb("away", [P, QUAD])
        step = sb("step", [P, QUAD])
        target = [sb(f"target{h}", [P, QUAD]) for h in range(2)]
        p_key = [ps(f"p_key{h}", [P, QUAD, P]) for h in range(2)]
        p_sum = [ps(f"p_sum{h}", [P, QUAD, P]) for h in range(2)]

        s_gidx = sem("gidx")
        s_rows = [own_sem(f"rows{h}") for h in range(2)]
        s_keys = sem("keys")
        s_prow = sem("prow")
        s_same = sem("same")
        s_cnt = sem("cnt")
        s_sidx = sem("sidx")
        s_sum = sem("sum")
        s_total = sem("total")
        s_added = [own_sem(f"added{j}") for j in range(QUAD)]
        s_zero = sem("zero")
        s_turn = sem("turn")
        if kind == "rel":
            s_mask = sem("mask")
            s_z = sem("z")
            s_zt = sem("zt")
            s_ztb = sem("ztb")
            mask = [sb(f"mask{h}", [P, QUAD, REL]) for h in range(2)]
            z = [sb(f"z{j}", [P, REL, D]) for j in range(QUAD)]
            ztb = [sb(f"ztb{h}", [P, QUAD, P]) for h in range(2)]
            p_zt = [ps(f"p_zt{h}", [P, QUAD, P]) for h in range(2)]
        if kind == "mlp":
            s_ew = [sem(f"ew{h}") for h in range(2)]
            s_pt = sem("pt")
            s_ht = sem("ht")
            s_p1 = sem("p1")
            s_e1 = sem("e1")
            s_p2 = sem("p2")
            s_e2 = sem("e2")
            ew = [sb(f"ew{h}", [1, QE]) for h in range(2)]
            ht = sb("ht", [P, QE])
            e1 = sb("e1", [P, QE])
            e2 = sb("e2", [P, QUAD, HID])
            biased = sb("biased", [P, QUAD, HID])
            s_b2 = sem("b2")
            p_t = ps("p_t", [P, QE])
            p_1 = ps("p_1", [P, QE])
            p_2 = ps("p_2", [P, QUAD, HID])
        if degrees:
            s_hot = sem("hot")
            s_deg = sem("deg")
            s_root = sem("root")
            hot_high = [sb(f"hot_high{h}", [P, QUAD, P], F16) for h in range(2)]
            hot_low = [sb(f"hot_low{h}", [P, QUAD, T], F16) for h in range(2)]
            p_deg = ps("p_deg", [P, 512])
        inner = ctx.enter_context(ExitStack())
        block = inner.enter_context(nc.Block())

        def scattered(eng, q):
            for j in range(QUAD):
                eng.wait_ge(s_added[j], 16 * (q - 1))

        @block.sync
        def _(sp):
            def clear_piece(i):
                for table in zero:
                    flat = table.rearrange("(p t) f -> p (t f)", p=P)
                    piece = flat.shape[1] // (ROUNDS - 1)
                    sp.dma_start(flat[:, bass.ds(i * piece, piece)], K["zero"][:, 0:piece]).then_inc(s_zero, 16)

            def load_weights(q, h, part):
                sp.dma_start(ew[h][0:1, 0:part],
                             weights["ew"][bass.ds(q * QE, part)].rearrange("(a n) -> a n", a=1)
                             ).then_inc(s_ew[h], 16)

            def body(i, first, last):
                for h in range(2):
                    q = i * 2 + h
                    if kind == "mlp":
                        if not first:
                            sp.wait_ge(s_p1, q - 1)
                        load_weights(q, h, RESTQ if last and h == 1 else QE)
                    if zero and h == 1 and not last:
                        if not first:
                            sp.wait_ge(s_sum, q - 2)
                        clear_piece(i)

            if zero or kind == "mlp":
                rounds(sp, ROUNDS, body)
            if zero:
                sp.wait_ge(s_zero, 16 * len(zero) * (ROUNDS - 1))

        @block.gpsimd
        def _(pool):
            def gather_tile(h, j):
                for g, (table, _) in enumerate(sources):
                    pool.indirect_dma_start(
                        out=rows[h][:, j, g * D:(g + 1) * D], out_offset=None, in_=table,
                        in_offset=bass.IndirectOffsetOnAxis(ap=gidx[g][h][:, j:j + 1], axis=0)
                    ).then_inc(s_rows[h], 16)

            def scatter_tile(q, h, j, first):
                if j >= nt:
                    pool.wait_ge(s_added[j - nt], 16 * (q + 1))
                elif not first:
                    pool.wait_ge(s_added[j - nt + QUAD], 16 * q)
                pool.sem_inc(s_turn, 1)
                pool.indirect_dma_start(
                    out=sums[j % nt],
                    out_offset=bass.IndirectOffsetOnAxis(ap=sidx[h][:, j:j + 1], axis=0),
                    in_=total[h][:, j, :], in_offset=None, compute_op=ALU.add
                ).then_inc(s_added[j], 16)

            for h in range(2):
                pool.wait_ge(s_gidx, h + 1)
                for j in range(QUAD):
                    gather_tile(h, j)

            def body(i, first, last):
                for h in range(2):
                    q = i * 2 + h
                    scatters = not (first and h == 0)
                    if scatters:
                        pool.wait_ge(s_sidx, q)
                        pool.wait_ge(s_total, q)
                    if not last:
                        pool.wait_ge(s_gidx, q + 3)
                        if kind == "rel":
                            pool.wait_ge(s_z, 4 * q + 4)
                        elif kind == "mlp":
                            pool.wait_ge(s_pt, q + 1)
                        else:
                            pool.wait_ge(s_sum, q + 1)
                        if not scatters:
                            pool.sem_inc(s_turn, 1)
                    for j in range(QUAD):
                        if scatters:
                            scatter_tile(q - 1, 1 - h, j, first and h == 1)
                        if not last:
                            gather_tile(h, j)

            rounds(pool, ROUNDS, body)
            pool.wait_ge(s_sidx, QUADS)
            pool.wait_ge(s_total, QUADS)
            for j in range(QUAD):
                scatter_tile(QUADS - 1, 1, j, False)
            for j in range(QUAD):
                pool.wait_ge(s_added[j], 16 * QUADS)

        landed = 16 * QUAD * ng

        @block.vector
        def _(dve):
            def stage_gather(q, h):
                for g, (_, index) in enumerate(sources):
                    last = nc.vector.tensor_copy(gidx[g][h][:, :], index[:, :, q])
                last.then_inc(s_gidx, 1)

            def hand_over(q, h, fresh):
                dve.wait_ge(s_cnt, 7 * q + 7)
                if not fresh:
                    scattered(dve, q)
                nc.vector.tensor_copy(sidx[h][:, :], target[h][:, :]).then_inc(s_sidx, 1)
                if kind == "mlp":
                    dve.wait_ge(s_sum, q + 1)
                    nc.vector.tensor_copy(total[h][:, :, :], p_sum[h][:, :, 0:width]).then_inc(s_total, 1)

            for h in range(2):
                stage_gather(h, h)
            nc.vector.tensor_copy(keys[0][:, :], key[:, :, 0]).then_inc(s_keys, 1)

            def body(i, first, last):
                for h in range(2):
                    q = i * 2 + h
                    if not (last and h == 1):
                        if not (first and h == 0):
                            dve.wait_ge(s_prow, q)
                            dve.wait_ge(s_cnt, q * 7)
                        nc.vector.tensor_copy(keys[1 - h][:, :], key[:, :, q + 1]).then_inc(s_keys, 1)
                    dve.wait_ge(s_prow, q + 1)
                    dve.wait_ge(s_keys, q + 1)
                    if not first:
                        dve.wait_ge(s_sum, q - 1)
                    nc.vector.tensor_tensor(same[h][:, :, :], p_key[h][:, :, :],
                                            bc(keys[h][:, :].unsqueeze(2), [P, QUAD, P]),
                                            ALU.is_equal).then_inc(s_same, 1)
                    dve.wait_ge(s_same, q + 1)
                    for j in range(QUAD):
                        if j:
                            dve.wait_ge(s_cnt, q * 7 + j)
                        nc.vector.tensor_tensor_reduce(
                            out=scratch[:, :], in0=same[h][:, j, :], in1=K["before"][:, :], scale=1.0,
                            scalar=0.0, op0=ALU.mult, op1=ALU.add, accum_out=earlier[:, j:j + 1]
                        ).then_inc(s_cnt, 1)
                    nc.vector.tensor_scalar(away[:, :], keys[h][:, :], -1.0, K["spare"][:, 0:1],
                                            ALU.mult, ALU.add).then_inc(s_cnt, 1)
                    dve.wait_ge(s_cnt, q * 7 + 5)
                    nc.vector.scalar_tensor_tensor(out=step[:, :], in0=earlier[:, :], scalar=0.5,
                                                   in1=away[:, :], op0=ALU.is_gt, op1=ALU.mult
                                                   ).then_inc(s_cnt, 1)
                    dve.wait_ge(s_cnt, q * 7 + 6)
                    nc.vector.tensor_tensor(target[h][:, :], step[:, :], keys[h][:, :], ALU.add
                                            ).then_inc(s_cnt, 1)
                    dve.wait_ge(s_rows[h], (i + 1) * landed)
                    if not last:
                        stage_gather(q + 2, h)
                    if degrees:
                        if not first:
                            dve.wait_ge(s_deg, q - 1)
                        one_hot(nc, K, K["high_dst"], K["low_dst"], bass.ds(q, 1), hot_high[h], hot_low[h]
                                ).then_inc(s_hot, 1)
                    if kind == "rel":
                        nc.vector.tensor_tensor(mask[h][:, :, :],
                                                bc(K["iota"][:, 0:REL].unsqueeze(1), [P, QUAD, REL]),
                                                bc(K["rel"][:, :, q].unsqueeze(2), [P, QUAD, REL]),
                                                ALU.is_equal).then_inc(s_mask, 1)
                        dve.wait_ge(s_mask, q + 1)
                        for j in range(QUAD):
                            if not (first and h == 0):
                                dve.wait_ge(s_zt, 4 * q + j - 3)
                            nc.vector.tensor_tensor(z[j][:, :, :],
                                                    bc(rows[h][:, j, :].unsqueeze(1), [P, REL, D]),
                                                    bc(mask[h][:, j, :].unsqueeze(2), [P, REL, D]),
                                                    ALU.mult).then_inc(s_z, 1)
                    if kind == "mlp":
                        dve.wait_ge(s_p2, q + 1)
                        if not (first and h == 0):
                            dve.wait_ge(s_e2, q)
                        nc.vector.tensor_tensor(biased[:, :, :], p_2[:, :, :],
                                                bc(weights["b2"][:, :].unsqueeze(1), [P, QUAD, HID]),
                                                ALU.add).then_inc(s_b2, 1)
                    if not (first and h == 0):
                        hand_over(q - 1, 1 - h, first)

            rounds(dve, ROUNDS, body)
            hand_over(QUADS - 1, 1, False)
            if degrees:
                dve.wait_ge(s_deg, QUADS)
                nc.vector.tensor_scalar(K["dinv"][:, :], p_deg[:, 0:T], 1.0, None, ALU.add).then_inc(s_root, 1)
                dve.wait_ge(s_root, 2)
                nc.vector.reciprocal(K["dinv"][:, :], K["dinv"][:, :])

        @block.tensor
        def _(pe):
            def spread(h):
                for j in range(QUAD):
                    last = nc.tensor.matmul(p_key[h][:, j, :], bc(keys[h][:, j:j + 1], [P, P]),
                                            K["ident"][:, :], start=True, stop=True)
                last.then_inc(s_prow, 1)

            pe.wait_ge(s_keys, 1)
            spread(0)

            def body(i, first, last):
                for h in range(2):
                    q = i * 2 + h
                    if not (last and h == 1):
                        pe.wait_ge(s_keys, q + 2)
                        if not (first and h == 0):
                            pe.wait_ge(s_same, q)
                        spread(1 - h)
                    pe.wait_ge(s_rows[h], (i + 1) * landed)
                    if kind == "mlp":
                        if not (first and h == 0):
                            pe.wait_ge(s_ht, q)
                        for j in range(QUAD):
                            last_mm = flip128(nc, p_t[:, j * P:(j + 1) * P], rows[h][:, j, :],
                                                          K["ident"][:, :])
                        last_mm.then_inc(s_pt, 1)
                        pe.wait_ge(s_ht, q + 1)
                        pe.wait_ge(s_ew[h], 16 * (i + 1))
                        if not (first and h == 0):
                            pe.wait_ge(s_e1, q)
                        nc.tensor.matmul(p_1[:, :], weights["W1"][:, :], ht[:, :], start=True, stop=False)
                        nc.tensor.matmul(p_1[:, :], weights["w1d"][:, :], ew[h][:, :], start=False,
                                         stop=True).then_inc(s_p1, 1)
                        pe.wait_ge(s_e1, q + 1)
                        if not (first and h == 0):
                            pe.wait_ge(s_b2, q)
                        for j in range(QUAD):
                            last_mm = nc.tensor.matmul(p_2[:, j, :], e1[:, j * P:(j + 1) * P],
                                                       weights["W2"][:, :], start=True, stop=True)
                        last_mm.then_inc(s_p2, 1)
                        pe.wait_ge(s_e2, q + 1)
                    pe.wait_ge(s_same, q + 1)
                    if not first:
                        pe.wait_ge(s_total, q - 1)
                    if kind == "rel":
                        def finish(j):
                            pe.wait_ge(s_ztb, 4 * q + j + 1)
                            for c in range(4):
                                mm = nc.tensor.matmul(p_sum[h][:, j, 0:D], ztb[j % 2][:, c, :],
                                                      weights["W"][:, c, :], start=c == 0, stop=c == 3)
                            return mm
                        for j in range(QUAD):
                            pe.wait_ge(s_z, 4 * q + j + 1)
                            if not (first and h == 0 and j < 2):
                                pe.wait_ge(s_ztb, 4 * q + j - 1)
                            for c in range(4):
                                mm = nc.tensor.matmul(
                                    p_zt[j % 2][:, c, :],
                                    z[j][:, 2 * c:2 * c + 2, :].rearrange("p r f -> p (r f)"),
                                    same[h][:, j, :], start=True, stop=True)
                            mm.then_inc(s_zt, 1)
                            if j:
                                finish(j - 1)
                        finish(QUAD - 1).then_inc(s_sum, 1)
                    else:
                        if degrees:
                            pe.wait_ge(s_hot, q + 1)
                            for j in range(QUAD):
                                mm = nc.tensor.matmul(p_deg[:, 0:T], hot_high[h][:, j, :], hot_low[h][:, j, :],
                                                      start=first and h == 0 and j == 0,
                                                      stop=last and h == 1 and j == QUAD - 1)
                            mm.then_inc(s_deg, 1)
                        message = e2 if kind == "mlp" else rows[h]
                        for j in range(QUAD):
                            mm = nc.tensor.matmul(p_sum[h][:, j, 0:width], same[h][:, j, :],
                                                  message[:, j, :], start=True, stop=True)
                        mm.then_inc(s_sum, 1)

            rounds(pe, ROUNDS, body)

        @block.scalar
        def _(act):
            def hand_over(q, h, fresh):
                act.wait_ge(s_sum, q + 1)
                if not fresh:
                    scattered(act, q)
                nc.scalar.copy(total[h][:, :, :], p_sum[h][:, :, 0:width]).then_inc(s_total, 1)

            def body(i, first, last):
                for h in range(2):
                    q = i * 2 + h
                    if kind == "rel":
                        for j in range(QUAD):
                            act.wait_ge(s_zt, 4 * q + j + 1)
                            nc.scalar.copy(ztb[j % 2][:, :, :], p_zt[j % 2][:, :, :]).then_inc(s_ztb, 1)
                    if kind == "mlp":
                        act.wait_ge(s_pt, q + 1)
                        if not (first and h == 0):
                            act.wait_ge(s_p1, q)
                        nc.scalar.copy(ht[:, :], p_t[:, :]).then_inc(s_ht, 1)
                        act.wait_ge(s_p1, q + 1)
                        if not (first and h == 0):
                            act.wait_ge(s_p2, q)
                        nc.scalar.activation(e1[:, :], p_1[:, :], ACT.Silu,
                                             bias=weights["b1"][:, 0:1]).then_inc(s_e1, 1)
                        act.wait_ge(s_b2, q + 1)
                        if not (first and h == 0):
                            act.wait_ge(s_sum, q)
                        nc.scalar.activation(e2[:, :, :], biased[:, :, :], ACT.Silu).then_inc(s_e2, 1)
                    if kind != "mlp" and not (first and h == 0):
                        hand_over(q - 1, 1 - h, first)

            rounds(act, ROUNDS, body)
            if kind != "mlp":
                hand_over(QUADS - 1, 1, False)
            if degrees:
                act.wait_ge(s_root, 1)
                nc.scalar.activation(K["dinv"][:, :], K["dinv"][:, :], ACT.Sqrt).then_inc(s_root, 1)

        inner.close()
        clear(nc, sems)


def prepare(nc, K, src, dst, rel, x, xp, y0, sums):
    with ExitStack() as ctx:
        def sb(name, shape, dt=F32):
            return ctx.enter_context(nc.sbuf_tensor(f"pre_{name}", shape, dt))

        sems = []

        def sem(name):
            sems.append(ctx.enter_context(nc.semaphore(f"pre_{name}")))
            return sems[-1]

        lists = (("src", src, PADKEY), ("dst", dst, PADKEY), ("rel", rel, 0))
        raw = [sb(f"raw_{n}", [QUADS, QE], I32) for n, _, _ in lists]
        rawf = [sb(f"rawf_{n}", [QUADS, QE]) for n, _, _ in lists]
        high = [sb("high_src", [P, QUAD, QUADS]), K["high_dst"]]
        low = [sb("low_src", [P, QUAD, QUADS]), K["low_dst"]]
        highi = sb("highi", [P, QUAD, QUADS], I32)
        below = sb("below", [P, QUAD, QUADS])
        iotai = sb("iotai", [P, T], I32)
        iota16 = K["iota16"]
        sparei = sb("sparei", [P, 1], I32)
        hot_high = [sb(f"hot_high{h}", [P, QUAD, P], F16) for h in range(2)]
        hot_low = [sb(f"hot_low{h}", [P, QUAD, T], F16) for h in range(2)]
        xall = sb("xall", [P, T, D])
        present = sb("present", [P, T])
        p_t = [ctx.enter_context(nc.psum_tensor(f"pre_p_t{k}", [P, QUAD, P], F32)) for k in range(3)]
        p_deg = ctx.enter_context(nc.psum_tensor("pre_p_deg", [P, 512], F32))

        s_padded = sem("padded")
        s_raw = sem("raw")
        s_x = sem("x")
        s_xp = sem("xp")
        s_y = sem("y")
        s_y0 = sem("y0")
        s_zero = sem("zero")
        s_clear = sem("clear")
        s_weights = sem("weights")
        s_inc = sem("inc")
        s_const = sem("const")
        s_rawf = sem("rawf")
        s_pt = sem("pt")
        s_v = sem("v")
        s_hot = sem("hot")
        s_deg = sem("deg")
        s_max = sem("max")
        s_root = sem("root")
        inner = ctx.enter_context(ExitStack())
        block = inner.enter_context(nc.Block())

        @block.gpsimd
        def _(pool):
            nc.gpsimd.memset(K["ident"][:, :], 0.0).then_inc(s_const, 1)
            nc.gpsimd.memset(K["before"][:, :], 1.0).then_inc(s_const, 1)
            pool.wait_ge(s_const, 2)
            nc.gpsimd.affine_select(out=K["ident"][:, :], in_=K["ident"][:, :],
                                    compare_op=ALU.not_equal, fill=1.0, base=0, pattern=[[-1, P]],
                                    channel_multiplier=1).then_inc(s_const, 1)
            nc.gpsimd.affine_select(out=K["before"][:, :], in_=K["before"][:, :],
                                    compare_op=ALU.is_gt, fill=0.0, base=0, pattern=[[-1, P]],
                                    channel_multiplier=1).then_inc(s_const, 1)
            nc.gpsimd.iota(iotai[:, :], [[1, T]], base=0, channel_multiplier=0).then_inc(s_const, 1)
            nc.gpsimd.iota(sparei[:, :], [[1, 1]], base=NR, channel_multiplier=1).then_inc(s_const, 1)

        @block.sync
        def _(sp):
            sp.wait_ge(s_padded, 4)
            for n, (_, a, _) in enumerate(lists):
                sp.dma_start(raw[n][0:96, :], a[0:96 * QE].rearrange("(q e) -> q e", e=QE)).then_inc(s_raw, 16)
                sp.dma_start(raw[n][96:97, :], a[96 * QE:97 * QE].rearrange("(q e) -> q e", e=QE)).then_inc(s_raw, 16)
                sp.dma_start(raw[n][97:98, 0:RESTQ], a[97 * QE:N].rearrange("(q e) -> q e", q=1)).then_inc(s_raw, 16)
            full = x[0:LASTP * T, :].rearrange("(p t) f -> p (t f)", p=LASTP)
            rows = xall[:, :, :].rearrange("p t f -> p (t f)")
            for a in range(0, T * D, XW):
                for p0, p1 in ((0, 112), (112, LASTP)):
                    sp.dma_start(rows[p0:p1, a:a + XW], full[p0:p1, a:a + XW]).then_inc(s_x, 16)
            sp.dma_start(rows[LASTP:P, 0:LASTT * D],
                         x[LASTP * T:N, :].rearrange("(a n) f -> a (n f)", a=1)).then_inc(s_x, 16)
            sp.wait_ge(s_x, 16 * (2 * XPARTS + 1))
            to = xp.rearrange("(p t) f -> p (t f)", p=P)
            for n in range(XPARTS):
                sp.dma_start(to[:, n * XW:(n + 1) * XW], rows[:, n * XW:(n + 1) * XW]).then_inc(s_xp, 16)
            sp.wait_ge(s_zero, 1)
            for table in sums:
                flat = table.rearrange("(p t) f -> p (t f)", p=P)
                for a in range(0, flat.shape[1], PIECE):
                    sp.dma_start(flat[:, a:a + PIECE], K["zero"][:, :]).then_inc(s_clear, 16)
            to = y0.rearrange("(p t) f -> p (t f)", p=P)
            for n in range(XPARTS):
                sp.wait_ge(s_y, n + 1)
                sp.dma_start(to[:, n * XW:(n + 1) * XW], rows[:, n * XW:(n + 1) * XW]).then_inc(s_y0, 16)
            sp.wait_ge(s_y0, 16 * XPARTS)
            sp.wait_ge(s_clear, 16 * len(sums) * (NA * D // P // PIECE))

        @block.vector
        def _(dve):
            for n, (_, _, pad) in enumerate(lists):
                nc.vector.memset(raw[n][:, :], pad).then_inc(s_padded, 1)
            nc.vector.memset(xall[96:P, LASTT:T, :], 0.0).then_inc(s_padded, 1)
            nc.vector.memset(K["zero"][:, :], 0.0).then_inc(s_zero, 1)
            nc.vector.memset(K["eps"][:, :], EPS)
            dve.wait_ge(s_raw, 16 * 9)
            for n in range(3):
                nc.vector.tensor_copy(rawf[n][:, :], raw[n][:, :]).then_inc(s_rawf, 1)
            dve.wait_ge(s_const, 6)
            nc.vector.tensor_copy(K["iota"][:, :], iotai[:, :])
            nc.vector.tensor_copy(iota16[:, :], iotai[:, :])
            nc.vector.tensor_copy(K["spare"][:, :], sparei[:, :])
            v = 0
            for n, name in enumerate(("src", "dst", "rel")):
                dve.wait_ge(s_pt, n + 1)
                nc.vector.tensor_copy(K[name][:, :, :], p_t[n][:, :, 0:QUADS]).then_inc(s_v, 1)
                v += 1
                if n < 2:
                    nc.vector.tensor_copy(K[name + "i"][:, :, :], p_t[n][:, :, 0:QUADS]).then_inc(s_v, 1)
                    v += 1
                    dve.wait_ge(s_v, v)
                    nc.vector.tensor_scalar(highi[:, :, :], K[name][:, :, :], 1.0 / T, 0.5 / T,
                                            ALU.mult, ALU.add).then_inc(s_v, 1)
                    dve.wait_ge(s_v, v + 1)
                    nc.vector.tensor_copy(high[n][:, :, :], highi[:, :, :]).then_inc(s_v, 1)
                    dve.wait_ge(s_v, v + 2)
                    nc.vector.scalar_tensor_tensor(out=low[n][:, :, :], in0=high[n][:, :, :],
                                                   scalar=float(-T), in1=K[name][:, :, :],
                                                   op0=ALU.mult, op1=ALU.add).then_inc(s_v, 1)
                    dve.wait_ge(s_v, v + 3)
                    nc.vector.tensor_scalar(below[:, :, :], low[n][:, :, :], 0.0, None, ALU.is_lt
                                            ).then_inc(s_v, 1)
                    dve.wait_ge(s_v, v + 4)
                    nc.vector.tensor_tensor(high[n][:, :, :], high[n][:, :, :], below[:, :, :],
                                            ALU.subtract).then_inc(s_v, 1)
                    nc.vector.scalar_tensor_tensor(out=low[n][:, :, :], in0=below[:, :, :],
                                                   scalar=float(T), in1=low[n][:, :, :],
                                                   op0=ALU.mult, op1=ALU.add).then_inc(s_v, 1)
                    v += 6
            dve.wait_ge(s_v, v)

            def body(i, first, last):
                for h in range(2):
                    q = i * 2 + h
                    if not first:
                        dve.wait_ge(s_deg, q - 1)
                    one_hot(nc, K, high[0], low[0], bass.ds(q, 1), hot_high[h], hot_low[h]).then_inc(s_hot, 1)

            rounds(dve, ROUNDS, body)
            dve.wait_ge(s_deg, QUADS)
            nc.vector.tensor_scalar(present[:, :], p_deg[:, 0:T], 0.5, None, ALU.is_gt).then_inc(s_v, 1)
            nc.vector.tensor_scalar(K["dis"][:, :], p_deg[:, 0:T], 1.0, None, ALU.max).then_inc(s_max, 1)
            dve.wait_ge(s_root, 1)
            nc.vector.reciprocal(K["dis"][:, :], K["dis"][:, :]).then_inc(s_v, 1)
            dve.wait_ge(s_v, v + 2)
            nc.vector.tensor_tensor(K["dis"][:, :], K["dis"][:, :], present[:, :], ALU.mult).then_inc(s_v, 1)
            dve.wait_ge(s_v, v + 3)
            dve.wait_ge(s_xp, 16 * XPARTS)
            for n in range(XPARTS):
                part = xall[:, n * XC:(n + 1) * XC, :]
                nc.vector.tensor_tensor(part, part, bc(K["dis"][:, n * XC:(n + 1) * XC].unsqueeze(2), [P, XC, D]),
                                        ALU.mult).then_inc(s_y, 1)
            resn, rese, inc = K["residuals"]
            nc.vector.tensor_copy(resn[0:D, :], K["ident"][0:D, 0:D])
            nc.vector.tensor_copy(inc[0:D, :], K["ident"][0:D, 0:D]).then_inc(s_inc, 1)
            dve.wait_ge(s_inc, 1)
            dve.wait_ge(s_weights, 16 * len(K["loads"]))
            nc.vector.tensor_tensor(rese[:, :], rese[:, :], inc[:, :], ALU.add)

        @block.tensor
        def _(pe):
            pe.wait_ge(s_const, 6)
            for n in range(3):
                pe.wait_ge(s_rawf, n + 1)
                for j in range(QUAD):
                    mm = flip128(nc, p_t[n][:, j, 0:QUADS], rawf[n][:, j * P:(j + 1) * P],
                                             K["ident"][0:QUADS, 0:QUADS])
                mm.then_inc(s_pt, 1)

            def body(i, first, last):
                for h in range(2):
                    q = i * 2 + h
                    pe.wait_ge(s_hot, q + 1)
                    for j in range(QUAD):
                        mm = nc.tensor.matmul(p_deg[:, 0:T], hot_high[h][:, j, :], hot_low[h][:, j, :],
                                              start=first and h == 0 and j == 0,
                                              stop=last and h == 1 and j == QUAD - 1)
                    mm.then_inc(s_deg, 1)

            rounds(pe, ROUNDS, body)

        @block.scalar
        def _(act):
            for to, of in K["loads"]:
                act.dma_start(to, of).then_inc(s_weights, 16)
            act.wait_ge(s_max, 1)
            nc.scalar.activation(K["dis"][:, :], K["dis"][:, :], ACT.Sqrt).then_inc(s_root, 1)

        inner.close()
        clear(nc, sems)


def node_pass(nc, label, K, kind, ins, outs, weights=None, copy=None):
    dense = kind in ("mlp", "conv1", "conv2")
    conv = kind in ("conv1", "conv2")
    normed = kind != "conv1"
    wide = kind in ("mlp", "conv2")
    NQ = CH // QUAD
    NS = 2 * NQ
    with ExitStack() as ctx:
        def sb(name, shape, dt=F32):
            return ctx.enter_context(nc.sbuf_tensor(f"{label}_{name}", shape, dt))

        def ps(name, shape):
            return ctx.enter_context(nc.psum_tensor(f"{label}_{name}", shape, F32))

        sems = []

        def sem(name):
            sems.append(K["semaphore"](f"node_{name}"))
            return sems[-1]

        widths = [t.shape[1] for t in ins]
        got = [[sb(f"in{n}_{h}", [P, CH, w]) for h in range(2)] for n, w in enumerate(widths)]
        result = [[sb(f"out{n}_{h}", [P, CH, D]) for h in range(2)] for n in range(len(outs))]
        value = [sb(f"value{h}", [P, CH, D]) for h in range(2)]
        s_in = [sem(f"in{h}") for h in range(2)]
        s_late = [sem(f"late{h}") for h in range(2)]
        s_out = [sem(f"out{h}") for h in range(2)]
        s_turn = sem("turn")
        s_tail = sem("tail")
        s_done = sem("done")
        s_v = sem("v")
        s_w = sem("w")
        s_value = sem("value")
        s_c = sem("c")
        s_sq = sem("sq")
        s_var = sem("var")
        s_std = sem("std")
        s_x3 = sem("x3")
        cent = sb("cent", [P, CH, D])
        sq = sb("sq", [P, CH, D])
        mean = sb("mean", [P, CH])
        var = sb("var", [P, CH])
        std = sb("std", [P, CH])
        rstd = sb("rstd", [P, CH])
        if dense:
            s_ones = sem("ones")
            s_z = sem("z")
            s_pt = sem("pt")
            s_t = sem("t")
            s_p = sem("p")
            s_u = sem("u")
            s_q = sem("q")
            s_o = sem("o")
            z = [sb(f"z{h}", [P, CH, D]) for h in range(2)] if conv else None
            flat_a = [sb(f"flat_a{n}", [P, QE]) for n in range(NQ)] if wide else None
            flat_x = [sb(f"flat_x{n}", [D + 1, QE]) for n in range(NQ)]
            p_a = [ps(f"p_a{b}", [P, QE]) for b in range(2)] if wide else None
            p_x = [ps(f"p_x{b}", [P, QE]) for b in range(2)]
            p_o = [ps(f"p_o{b}", [P, QUAD, P]) for b in range(2)]
            if kind == "mlp":
                u = [sb(f"u{b}", [P, QE]) for b in range(2)]
                p_1 = [ps(f"p_1{b}", [P, QE]) for b in range(2)]
        inner = ctx.enter_context(ExitStack())
        block = inner.enter_context(nc.Block())
        stores = 3 if kind == "conv2" else len(outs) + (copy is not None)
        late = 1 if kind == "conv2" else 0
        early = len(ins) - late

        def place(i, k):
            return i * NS + k, i * 2 + k // NQ, (k // NQ) % 2, k % 2, k % NQ

        @block.sync
        def _(sp):
            def load(c, h, of, signal):
                for n in of:
                    w = widths[n]
                    sp.dma_start(got[n][h][:, :, :].rearrange("p t f -> p (t f)"),
                                 ins[n][0:NR, :].rearrange("(p t) f -> p (t f)", p=P)[:, bass.ds(c * (CH * w), CH * w)]
                                 ).then_inc(signal[h], 16)

            def store(c, h):
                sp.wait_ge(s_done, c + 1)
                for n, table in enumerate(outs):
                    of = result[n][h][:, :, :].rearrange("p t f -> p (t f)")
                    if kind != "conv2":
                        sp.dma_start(chunk_of(table, c), of).then_inc(s_out[h], 16)
                        continue
                    full, tail = table
                    to = full[0:LASTP * T, :].rearrange("(p t) f -> p (t f)", p=LASTP)
                    sp.dma_start(to[0:112, bass.ds(c * CW, CW)], of[0:112, :]).then_inc(s_out[h], 16)
                    sp.dma_start(to[112:LASTP, bass.ds(c * CW, CW)], of[112:LASTP, :]).then_inc(s_out[h], 16)
                    sp.dma_start(tail.rearrange("(a t) f -> a (t f)", a=1)[:, bass.ds(c * CW, CW)],
                                 of[LASTP:P, :]).then_inc(s_out[h], 16)
                if copy is not None:
                    sp.dma_start(chunk_of(copy, c), of).then_inc(s_out[h], 16)

            load(0, 0, range(early), s_in)
            load(0, 0, range(early, len(ins)), s_late)
            if copy is not None:
                sp.dma_start(copy[NR:NA, :], K["zero"][:, 0:D]).then_inc(s_tail, 16)

            def body(i, first, last):
                for h in range(2):
                    c = i * 2 + h
                    if not (last and h == 1):
                        if not (first and h == 0):
                            if kind == "mlp":
                                sp.wait_ge(s_pt, c * NQ)
                            elif conv:
                                sp.wait_ge(s_z, c)
                            else:
                                sp.wait_ge(s_value, c)
                        load(c + 1, 1 - h, range(early), s_in)
                        if late:
                            if not (first and h == 0):
                                sp.wait_ge(s_pt, c * NQ)
                            load(c + 1, 1 - h, range(early, len(ins)), s_late)
                    if not (first and h == 0):
                        store(c - 1, 1 - h)

            rounds(sp, CROUNDS, body)
            store(CHUNKS - 1, 1)
            for h in range(2):
                sp.wait_ge(s_out[h], 16 * stores * CROUNDS)
            if copy is not None:
                sp.wait_ge(s_tail, 16)
            if kind == "conv2":
                full, tail = outs[0]
                sp.dma_start(full[LASTP * T:N, :].rearrange("(a n) f -> a (n f)", a=8),
                             tail[0:LASTT, :].rearrange("(a n) f -> a (n f)", a=8)).then_inc(s_tail, 16)
                sp.wait_ge(s_tail, 16)

        @block.vector
        def _(dve):
            def scale_of(name, c):
                return bc(K[name][:, bass.ds(c * CH, CH)].unsqueeze(2), [P, CH, D])

            def before(i, k, first):
                c = i * 2 + k
                h = k % 2
                g = [got[n][h][:, :, :] for n in range(len(ins))]
                if kind == "mlp":
                    return
                dve.wait_ge(s_in[h], 16 * early * (i + k // 2 + 1))
                if kind == "norm0":
                    v = value[h][:, :, :]
                    nc.vector.tensor_tensor(v, g[1], g[2], ALU.add).then_inc(s_v, 1)
                    dve.wait_ge(s_v, 2 * c + 1)
                    nc.vector.tensor_tensor(v, v, scale_of("dis", c), ALU.mult).then_inc(s_v, 1)
                    dve.wait_ge(s_v, 2 * c + 2)
                    nc.vector.tensor_tensor(v, v, g[0], ALU.add).then_inc(s_value, 1)
                elif kind == "norm":
                    nc.vector.tensor_tensor(value[h][:, :, :], g[0], g[1], ALU.add).then_inc(s_value, 1)
                else:
                    if not (first and k < 2):
                        dve.wait_ge(s_pt, (c - 1) * NQ)
                    v = z[h][:, :, :]
                    nc.vector.tensor_tensor(v, g[0], g[1], ALU.add).then_inc(s_v, 1)
                    dve.wait_ge(s_v, c + 1)
                    nc.vector.tensor_tensor(v, v, scale_of("dinv", c), ALU.mult).then_inc(s_z, 1)

            def center(i, h):
                c = i * 2 + h
                if dense:
                    dve.wait_ge(s_o, (c + 1) * NQ)
                else:
                    dve.wait_ge(s_value, c + 1)
                nc.vector.tensor_reduce(mean[:, :], value[h][:, :, :], AX.X, ALU.add).then_inc(s_w, 1)
                dve.wait_ge(s_w, 3 * c + 1)
                nc.vector.tensor_scalar(mean[:, :], mean[:, :], 1.0 / D, None, ALU.mult).then_inc(s_w, 1)
                dve.wait_ge(s_w, 3 * c + 2)
                nc.vector.tensor_tensor(cent[:, :, :], value[h][:, :, :],
                                        bc(mean[:, :].unsqueeze(2), [P, CH, D]), ALU.subtract).then_inc(s_c, 1)

            def norm(i, h, first):
                c = i * 2 + h
                dve.wait_ge(s_sq, c + 1)
                nc.vector.tensor_reduce(var[:, :], sq[:, :, :], AX.X, ALU.add).then_inc(s_var, 1)
                dve.wait_ge(s_std, c + 1)
                nc.vector.reciprocal(rstd[:, :], std[:, :]).then_inc(s_w, 1)
                dve.wait_ge(s_w, 3 * c + 3)
                if not first:
                    dve.wait_ge(s_out[h], 16 * stores * i)
                op = nc.vector.tensor_tensor(result[0][h][:, :, :], cent[:, :, :],
                                             bc(rstd[:, :].unsqueeze(2), [P, CH, D]), ALU.mult)
                if kind == "mlp":
                    op.then_inc(s_x3, 1)
                    dve.wait_ge(s_x3, c + 1)
                    op = nc.vector.tensor_tensor(result[1][h][:, :, :], result[0][h][:, :, :],
                                                 scale_of("dinv", c), ALU.mult)
                op.then_inc(s_done, 1)

            if dense:
                for n in range(NQ):
                    op = nc.vector.memset(flat_x[n][D:D + 1, :], 1.0)
                op.then_inc(s_ones, 1)

            def body(i, first, last):
                for h in range(2):
                    c = i * 2 + h
                    if conv and not (last and h == 1):
                        before(i, h + 1, first)
                    if normed:
                        center(i, h)
                        if not dense and not (last and h == 1):
                            before(i, h + 1, first)
                        norm(i, h, first)
                    else:
                        dve.wait_ge(s_o, (c + 1) * NQ)
                        if not first:
                            dve.wait_ge(s_out[h], 16 * stores * i)
                        nc.vector.tensor_tensor(result[0][h][:, :, :], value[h][:, :, :],
                                                scale_of("dinv", c), ALU.mult).then_inc(s_done, 1)

            before(0, 0, True)
            rounds(dve, CROUNDS, body)

        @block.scalar
        def _(act):
            def square(c):
                act.wait_ge(s_c, c + 1)
                nc.scalar.activation(sq[:, :, :], cent[:, :, :], ACT.Square).then_inc(s_sq, 1)

            def root(c):
                act.wait_ge(s_var, c + 1)
                nc.scalar.activation(std[:, :], var[:, :], ACT.Sqrt, scale=1.0 / D,
                                     bias=K["eps"][:, 0:1]).then_inc(s_std, 1)

            def to_sbuf(i, k, first):
                m, c, h, b, n = place(i, k)
                act.wait_ge(s_pt, m + 1)
                if not (first and k < NQ):
                    act.wait_ge(s_q, m + 1 - NQ)
                if wide:
                    w = D if kind == "conv2" else P
                    nc.scalar.copy(flat_a[n][0:w, :], p_a[b][0:w, :])
                nc.scalar.copy(flat_x[n][0:D, :], p_x[b][0:D, :]).then_inc(s_t, 1)

            def out_of(i, k, first):
                m, c, h, b, n = place(i, k)
                act.wait_ge(s_q, m + 1)
                if n == 0 and not (first and k < NS):
                    act.wait_ge(s_c if normed else s_done, c - 1)
                nc.scalar.activation(value[h][:, n * QUAD:(n + 1) * QUAD, :], p_o[b][:, :, 0:D],
                                     ACT.Relu if kind == "conv1" else ACT.Copy).then_inc(s_o, 1)

            def body(i, first, last):
                if not dense:
                    for h in range(2):
                        square(i * 2 + h)
                        root(i * 2 + h)
                    return
                for k in range(NS):
                    m, c, h, b, n = place(i, k)
                    if not (last and k == NS - 1):
                        to_sbuf(i, k + 1, first)
                    if kind == "mlp":
                        act.wait_ge(s_p, m + 1)
                        if not (first and k < 2):
                            act.wait_ge(s_q, m - 1)
                        nc.scalar.activation(u[b][:, :], p_1[b][:, :], ACT.Silu,
                                             bias=weights["b1"][:, 0:1]).then_inc(s_u, 1)
                    if not (first and k == 0):
                        out_of(i, k - 1, first)
                    if normed and not (first and h == 0):
                        if n == 3:
                            square(c - 1)
                        if n == 5:
                            root(c - 1)

            if dense:
                to_sbuf(0, 0, True)
            rounds(act, CROUNDS, body)
            if dense:
                out_of(CROUNDS - 1, NS - 1, False)
                if normed:
                    square(CHUNKS - 1)
                    root(CHUNKS - 1)

        @block.tensor
        def _(pe):
            if not dense:
                return

            def flip(i, k, first):
                m, c, h, b, n = place(i, k)
                if n == 0:
                    if kind == "mlp":
                        pe.wait_ge(s_in[h], 16 * early * (i + k // NS + 1))
                    if late:
                        pe.wait_ge(s_late[h], 16 * late * (i + k // NS + 1))
                    if conv:
                        pe.wait_ge(s_z, c + 1)
                if not (first and k < 2):
                    pe.wait_ge(s_t, m - 1)
                pe.sem_inc(s_turn, 1)
                x_of = {"mlp": got[0], "conv1": z, "conv2": got[-1]}[kind]
                a_of = {"mlp": got[-1], "conv1": None, "conv2": z}[kind]
                for j in range(QUAD):
                    t = n * QUAD + j
                    if wide:
                        w = D if kind == "conv2" else P
                        flip128(nc, p_a[b][0:w, j * P:(j + 1) * P], a_of[h][:, t, :], K["ident"][:, :])
                    mm = flip128(nc, p_x[b][0:D, j * P:(j + 1) * P], x_of[h][:, t, :], K["ident"][:, :])
                mm.then_inc(s_pt, 1)

            def first_product(i, k, first):
                m, c, h, b, n = place(i, k)
                pe.wait_ge(s_t, m + 1)
                if not (first and k < 2):
                    pe.wait_ge(s_u, m - 1)
                nc.tensor.matmul(p_1[b][:, :], weights["Wa"][:, :], flat_a[n][:, :], start=True, stop=False)
                nc.tensor.matmul(p_1[b][:, :], weights["Wx"][:, :], flat_x[n][0:D, :], start=False,
                                 stop=True).then_inc(s_p, 1)

            def second_product(i, k, first):
                m, c, h, b, n = place(i, k)
                pe.wait_ge(s_t, m + 1)
                if kind == "mlp":
                    pe.wait_ge(s_u, m + 1)
                if not (first and k < 2):
                    pe.wait_ge(s_o, m - 1)
                for j in range(QUAD):
                    part = slice(j * P, (j + 1) * P)
                    mm = nc.tensor.matmul(p_o[b][:, j, 0:D], flat_x[n][0:D + 1, part],
                                          weights["res"][0:D + 1, :], start=True, stop=not wide)
                    if kind == "mlp":
                        mm = nc.tensor.matmul(p_o[b][:, j, 0:D], u[b][:, part], weights["W2"][:, :],
                                              start=False, stop=True)
                    elif kind == "conv2":
                        mm = nc.tensor.matmul(p_o[b][:, j, 0:D], flat_a[n][0:D, part], weights["W2"][0:D, :],
                                              start=False, stop=True)
                mm.then_inc(s_q, 1)

            def body(i, first, last):
                for k in range(NS):
                    if not (last and k == NS - 1):
                        flip(i, k + 1, first)
                    if kind == "mlp":
                        first_product(i, k, first)
                        if not (first and k == 0):
                            second_product(i, k - 1, first)
                    else:
                        second_product(i, k, first)

            pe.wait_ge(s_ones, 1)
            flip(0, 0, True)
            rounds(pe, CROUNDS, body)
            if kind == "mlp":
                second_product(CROUNDS - 1, NS - 1, False)

        inner.close()
        clear(nc, sems)


def gnn(nc, x, src, dst, rel, ew, W, eW1, eb1, eW2, eb2, nW1, nb1, nW2, nb2, W1, b1, W2, b2, We, be, out):
    def table(name, rows=NR, width=D):
        return nc.dram_tensor(name, [rows, width], F32, kind="Internal").ap()

    xp = table("x_padded")
    y0 = table("y0")
    x1 = table("x1")
    x2 = table("x2")
    x3 = table("x3")
    y3 = table("y3")
    y4 = table("y4")
    tail = table("out_tail", T)
    sums0 = [table(f"sums0_{n}", NA) for n in range(2)]
    sums1 = [table(f"sums1_{n}", NA) for n in range(2)]
    sums2 = [table("sums2", NA, HID)]
    sums3 = [table(f"sums3_{n}", NA) for n in range(2)]
    sums4 = [table(f"sums4_{n}", NA) for n in range(2)]
    with ExitStack() as ctx:
        def sb(name, shape, dt=F32):
            return ctx.enter_context(nc.sbuf_tensor(name, shape, dt))

        K = {name: sb(name, shape) for name, shape in (
            ("ident", [P, P]), ("before", [P, P]), ("iota", [P, T]), ("spare", [P, 1]), ("eps", [P, 1]),
            ("src", [P, QUAD, QUADS]), ("dst", [P, QUAD, QUADS]),
            ("rel", [P, QUAD, QUADS]), ("dis", [P, T]), ("dinv", [P, T]), ("zero", [P, PIECE]))}
        semaphores = {}

        def semaphore(name):
            if name not in semaphores:
                semaphores[name] = ctx.enter_context(nc.semaphore(name))
            return semaphores[name]

        K["semaphore"] = semaphore
        K["iota16"] = sb("iota16", [P, T], F16)
        K["high_dst"] = sb("high_dst", [P, QUAD, QUADS])
        K["low_dst"] = sb("low_dst", [P, QUAD, QUADS])
        K["srci"] = sb("srci", [P, QUAD, QUADS], I32)
        K["dsti"] = sb("dsti", [P, QUAD, QUADS], I32)
        wrel = sb("wrel", [P, 4, D])
        we1 = sb("we1", [P, HID])
        we1d = sb("we1d", [1, HID])
        we2 = sb("we2", [P, HID])
        be1 = sb("be1", [P, 1])
        be2 = sb("be2", [P, HID])
        wnx = sb("wnx", [D, HID])
        wna = sb("wna", [HID, HID])
        wn2 = sb("wn2", [HID, D])
        bn1 = sb("bn1", [P, 1])
        w1b = sb("w1b", [D + 1, D])
        w2 = sb("w2", [D, D])
        resn = sb("resn", [D + 1, D])
        rese = sb("rese", [D + 1, D])
        inc = sb("inc", [D + 1, D])
        K["residuals"] = (resn, rese, inc)

        def row(a):
            return a.rearrange("(a n) -> a n", a=1)

        def column(a):
            return a.rearrange("(n a) -> n a", a=1)

        loads = ((wrel[:, :, :], W.rearrange("(c r) i h -> (r i) c h", r=2)), (we1[:, :], eW1[0:2 * D, :]),
                 (we1d[:, :], eW1[2 * D:2 * D + 1, :]), (we2[:, :], eW2), (be1[:, :], column(eb1)),
                 (be2[:, :], eb2.partition_broadcast(P)), (wnx[:, :], nW1[0:D, :]), (wna[:, :], nW1[D:D + HID, :]),
                 (wn2[:, :], nW2), (bn1[:, :], column(nb1)), (w1b[0:D, :], W1), (w1b[D:D + 1, :], row(b1)),
                 (w2[:, :], W2), (resn[D:D + 1, :], row(nb2)), (rese[0:D, :], We), (rese[D:D + 1, :], row(b2)),
                 (inc[D:D + 1, :], row(be)))
        K["loads"] = loads

        prepare(nc, K, src, dst, rel, x, xp, y0, sums0)
        edge_pass(nc, "e0", K, [(y0, K["dsti"])], K["src"], sums0, D, "plain", zero=sums1[1:], degrees=True)
        node_pass(nc, "n1", K, "norm0", [xp] + sums0, [x1], copy=sums1[0])
        edge_pass(nc, "e1", K, [(x1, K["srci"])], K["dst"], sums1, D, "rel", zero=sums2, weights={"W": wrel})
        node_pass(nc, "n2", K, "norm", sums1, [x2])
        edge_pass(nc, "e2", K, [(x2, K["srci"]), (x2, K["dsti"])], K["src"], sums2, HID, "mlp",
                  zero=sums3[1:],
                  weights={"W1": we1, "w1d": we1d, "W2": we2, "b1": be1, "b2": be2, "ew": ew})
        node_pass(nc, "n3", K, "mlp", [x2] + sums2, [x3, y3], copy=sums3[0],
                  weights={"Wx": wnx, "Wa": wna, "W2": wn2, "b1": bn1, "res": resn})
        edge_pass(nc, "e3", K, [(y3, K["srci"])], K["dst"], sums3, D, "plain", zero=sums4[1:])
        node_pass(nc, "n4", K, "conv1", sums3, [y4], copy=sums4[0], weights={"res": w1b})
        edge_pass(nc, "e4", K, [(y4, K["srci"])], K["dst"], sums4, D, "plain")
        node_pass(nc, "n5", K, "conv2", sums4 + [x3], [(out, tail)], weights={"W2": w2, "res": rese})


_INS = ["x", "src", "dst", "edge_type_8", "edge_weight1", "L1_gnn_W", "L2_gnn_eW1", "L2_gnn_eb1",
        "L2_gnn_eW2", "L2_gnn_eb2", "L2_gnn_nW1", "L2_gnn_nb1", "L2_gnn_nW2", "L2_gnn_nb2",
        "L3_gnn_W1", "L3_gnn_b1", "L3_gnn_W2", "L3_gnn_b2", "L3_gnn_W_emb", "L3_gnn_b_emb"]


def kernel(**inputs):
    import numpy as _np
    import concourse.bacc as _bacc
    from concourse import mybir as _mybir
    from concourse.bass_utils import run_bass_kernel_spmd as _run

    nc = _bacc.Bacc("TRN2", target_bir_lowering=False, num_devices=1)
    arrays, args = {}, []
    for name in _INS:
        a = _np.ascontiguousarray(inputs[name])
        if name == "edge_weight1":
            a = a.reshape(-1)
        arrays[f"in_{name}"] = a
        args.append(nc.dram_tensor(f"in_{name}", a.shape, _mybir.dt.from_np(a.dtype), kind="ExternalInput").ap())
    args.append(nc.dram_tensor("out_x", (N, D), F32, kind="ExternalOutput").ap())
    gnn(nc, *args)
    r = _run(nc, [arrays], core_ids=[0])
    return r.results[0]["out_x"]
```

```python
import numpy as np
import concourse.bass as bass
from concourse import mybir
from contextlib import ExitStack

F32 = mybir.dt.float32
F16 = mybir.dt.float16
BF16 = mybir.dt.bfloat16
I32 = mybir.dt.int32
ALU = mybir.AluOpType
ACT = mybir.ActivationFunctionType
AX = mybir.AxisListType

P = 128
N = 50000
D = 64
HID = 128
REL = 8
QUAD = 4
QUADS = 98
ROUNDS = QUADS // 2
QE = QUAD * P
FULLQ = N // QE
RESTQ = N - FULLQ * QE
T = QUADS * QUAD
NR = P * T
PADKEY = NR - 1
NA = NR + P
CH = 28
CHUNKS = T // CH
CROUNDS = CHUNKS // 2
CW = CH * D
LASTP = P - 1
LASTT = N - LASTP * T
EPS = 1e-5
XPARTS = 8
XC = T // XPARTS
XW = XC * D
PIECE = NA * D // P // 8
HOTS = 2


def bc(ap, shape):
    return ap.to_broadcast(shape)


def flip128(nc, out, a, ident):
    return nc.tensor.matmul(out, a, ident, is_transpose=True, start=True, stop=True)


def clear(nc, sems):
    with nc.Block() as block:
        @block.gpsimd
        def _(pool):
            for s in sems:
                pool.sem_clear(s)


def rounds(eng, count, body, alone=1):
    for i in range(alone):
        body(i, i == 0, False)
    with eng.Fori(alone, count - 1) as i:
        body(i, False, False)
    body(count - 1, False, True)


def chunk_of(table, c):
    return table[0:NR, :].rearrange("(p t) f -> p (t f)", p=P)[:, bass.ds(c * CW, CW)]


def one_hot(nc, K, high, low, columns, hot_high, hot_low, lows=QUAD):
    for j in range(QUAD):
        op = nc.vector.tensor_scalar(hot_high[:, j, :], K["iota16"][:, 0:P], high[:, j, columns], None, ALU.is_equal)
        if j < lows:
            op = nc.vector.tensor_scalar(hot_low[:, j, :], K["iota16"][:, :], low[:, j, columns], None, ALU.is_equal)
    return op


def edge_pass(nc, label, K, sources, key, sums, width, kind, zero=(), weights=None, degrees=False):
    ng = len(sources)
    nt = len(sums)
    with ExitStack() as ctx:
        def sb(name, shape, dt=F32):
            return ctx.enter_context(nc.sbuf_tensor(f"{label}_{name}", shape, dt))

        def ps(name, shape):
            return ctx.enter_context(nc.psum_tensor(f"{label}_{name}", shape, F32))

        sems = []

        def sem(name):
            sems.append(K["semaphore"](f"edge_{name}"))
            return sems[-1]

        def own_sem(name):
            return K["semaphore"](f"{label}_{name}")

        gidx = [[sb(f"gidx{g}_{h}", [P, QUAD], I32) for h in range(2)] for g in range(ng)]
        rows = [sb(f"rows{h}", [P, QUAD, D * ng]) for h in range(2)]
        keys = [sb(f"keys{h}", [P, QUAD]) for h in range(2)]
        same = [sb(f"same{h}", [P, QUAD, P]) for h in range(2)]
        sidx = [sb(f"sidx{h}", [P, QUAD], I32) for h in range(2)]
        total = [sb(f"total{h}", [P, QUAD, width]) for h in range(2)]
        earlier = sb("earlier", [P, QUAD])
        scratch = sb("scratch", [P, P])
        away = sb("away", [P, QUAD])
        step = sb("step", [P, QUAD])
        target = [sb(f"target{h}", [P, QUAD]) for h in range(2)]
        p_key = [ps(f"p_key{h}", [P, QUAD, P]) for h in range(2)]
        p_sum = [ps(f"p_sum{h}", [P, QUAD, P]) for h in range(2)]

        s_gidx = sem("gidx")
        s_rows = [own_sem(f"rows{h}") for h in range(2)]
        s_keys = sem("keys")
        s_prow = sem("prow")
        s_same = sem("same")
        s_cnt = sem("cnt")
        s_sidx = sem("sidx")
        s_sum = sem("sum")
        s_total = sem("total")
        s_added = [own_sem(f"added{j}") for j in range(QUAD)]
        s_zero = sem("zero")
        s_turn = sem("turn")
        if kind == "rel":
            s_mask = sem("mask")
            s_z = sem("z")
            s_zt = sem("zt")
            s_ztb = sem("ztb")
            mask = [sb(f"mask{h}", [P, QUAD, REL]) for h in range(2)]
            z = [sb(f"z{j}", [P, REL, D]) for j in range(QUAD)]
            ztb = [sb(f"ztb{h}", [P, QUAD, P]) for h in range(2)]
            p_zt = [ps(f"p_zt{h}", [P, QUAD, P]) for h in range(2)]
        if kind == "mlp":
            s_ew = [sem(f"ew{h}") for h in range(2)]
            s_pt = sem("pt")
            s_ht = sem("ht")
            s_p1 = sem("p1")
            s_e1 = sem("e1")
            s_p2 = sem("p2")
            s_e2 = sem("e2")
            ew = [sb(f"ew{h}", [1, QE]) for h in range(2)]
            ht = sb("ht", [P, QE])
            e1 = sb("e1", [P, QE])
            e2 = sb("e2", [P, QUAD, HID])
            biased = sb("biased", [P, QUAD, HID])
            s_b2 = sem("b2")
            p_t = ps("p_t", [P, QE])
            p_1 = ps("p_1", [P, QE])
            p_2 = ps("p_2", [P, QUAD, HID])
        if degrees:
            s_hot = sem("hot")
            s_deg = sem("deg")
            s_root = sem("root")
            hot_high = [sb(f"hot_high{h}", [P, QUAD, P], F16) for h in range(2)]
            hot_low = [sb(f"hot_low{h}", [P, QUAD, T], F16) for h in range(2)]
            p_deg = ps("p_deg", [P, 512])
        inner = ctx.enter_context(ExitStack())
        block = inner.enter_context(nc.Block())

        def scattered(eng, q):
            for j in range(QUAD):
                eng.wait_ge(s_added[j], 16 * (q - 1))

        @block.sync
        def _(sp):
            def clear_piece(i):
                for table in zero:
                    flat = table.rearrange("(p t) f -> p (t f)", p=P)
                    piece = flat.shape[1] // (ROUNDS - 1)
                    sp.dma_start(flat[:, bass.ds(i * piece, piece)], K["zero"][:, 0:piece]).then_inc(s_zero, 16)

            def load_weights(q, h, part):
                sp.dma_start(ew[h][0:1, 0:part],
                             weights["ew"][bass.ds(q * QE, part)].rearrange("(a n) -> a n", a=1)
                             ).then_inc(s_ew[h], 16)

            def body(i, first, last):
                for h in range(2):
                    q = i * 2 + h
                    if kind == "mlp":
                        if not first:
                            sp.wait_ge(s_p1, q - 1)
                        load_weights(q, h, RESTQ if last and h == 1 else QE)
                    if zero and h == 1 and not last:
                        if not first:
                            sp.wait_ge(s_sum, q - 2)
                        clear_piece(i)

            if zero or kind == "mlp":
                rounds(sp, ROUNDS, body)
            if zero:
                sp.wait_ge(s_zero, 16 * len(zero) * (ROUNDS - 1))

        @block.gpsimd
        def _(pool):
            def gather_tile(h, j):
                for g, (table, _) in enumerate(sources):
                    pool.indirect_dma_start(
                        out=rows[h][:, j, g * D:(g + 1) * D], out_offset=None, in_=table,
                        in_offset=bass.IndirectOffsetOnAxis(ap=gidx[g][h][:, j:j + 1], axis=0)
                    ).then_inc(s_rows[h], 16)

            def scatter_tile(q, h, j, first):
                if j >= nt:
                    pool.wait_ge(s_added[j - nt], 16 * (q + 1))
                elif not first:
                    pool.wait_ge(s_added[j - nt + QUAD], 16 * q)
                pool.sem_inc(s_turn, 1)
                pool.indirect_dma_start(
                    out=sums[j % nt],
                    out_offset=bass.IndirectOffsetOnAxis(ap=sidx[h][:, j:j + 1], axis=0),
                    in_=total[h][:, j, :], in_offset=None, compute_op=ALU.add
                ).then_inc(s_added[j], 16)

            for h in range(2):
                pool.wait_ge(s_gidx, h + 1)
                for j in range(QUAD):
                    gather_tile(h, j)

            def body(i, first, last):
                for h in range(2):
                    q = i * 2 + h
                    scatters = not (first and h == 0)
                    if scatters:
                        pool.wait_ge(s_sidx, q)
                        pool.wait_ge(s_total, q)
                    if not last:
                        pool.wait_ge(s_gidx, q + 3)
                        if kind == "rel":
                            pool.wait_ge(s_z, 4 * q + 4)
                        elif kind == "mlp":
                            pool.wait_ge(s_pt, q + 1)
                        else:
                            pool.wait_ge(s_sum, q + 1)
                        if not scatters:
                            pool.sem_inc(s_turn, 1)
                    for j in range(QUAD):
                        if scatters:
                            scatter_tile(q - 1, 1 - h, j, first and h == 1)
                        if not last:
                            gather_tile(h, j)

            rounds(pool, ROUNDS, body)
            pool.wait_ge(s_sidx, QUADS)
            pool.wait_ge(s_total, QUADS)
            for j in range(QUAD):
                scatter_tile(QUADS - 1, 1, j, False)
            for j in range(QUAD):
                pool.wait_ge(s_added[j], 16 * QUADS)

        landed = 16 * QUAD * ng

        @block.vector
        def _(dve):
            def stage_gather(q, h):
                for g, (_, index) in enumerate(sources):
                    last = nc.vector.tensor_copy(gidx[g][h][:, :], index[:, :, q])
                last.then_inc(s_gidx, 1)

            def hand_over(q, h, fresh):
                dve.wait_ge(s_cnt, 7 * q + 7)
                if not fresh:
                    scattered(dve, q)
                nc.vector.tensor_copy(sidx[h][:, :], target[h][:, :]).then_inc(s_sidx, 1)
                if kind == "mlp":
                    dve.wait_ge(s_sum, q + 1)
                    nc.vector.tensor_copy(total[h][:, :, :], p_sum[h][:, :, 0:width]).then_inc(s_total, 1)

            for h in range(2):
                stage_gather(h, h)
            nc.vector.tensor_copy(keys[0][:, :], key[:, :, 0]).then_inc(s_keys, 1)

            def body(i, first, last):
                for h in range(2):
                    q = i * 2 + h
                    if not (last and h == 1):
                        if not (first and h == 0):
                            dve.wait_ge(s_prow, q)
                            dve.wait_ge(s_cnt, q * 7)
                        nc.vector.tensor_copy(keys[1 - h][:, :], key[:, :, q + 1]).then_inc(s_keys, 1)
                    dve.wait_ge(s_prow, q + 1)
                    dve.wait_ge(s_keys, q + 1)
                    if not first:
                        dve.wait_ge(s_sum, q - 1)
                    nc.vector.tensor_tensor(same[h][:, :, :], p_key[h][:, :, :],
                                            bc(keys[h][:, :].unsqueeze(2), [P, QUAD, P]),
                                            ALU.is_equal).then_inc(s_same, 1)
                    dve.wait_ge(s_same, q + 1)
                    for j in range(QUAD):
                        if j:
                            dve.wait_ge(s_cnt, q * 7 + j)
                        nc.vector.tensor_tensor_reduce(
                            out=scratch[:, :], in0=same[h][:, j, :], in1=K["before"][:, :], scale=1.0,
                            scalar=0.0, op0=ALU.mult, op1=ALU.add, accum_out=earlier[:, j:j + 1]
                        ).then_inc(s_cnt, 1)
                    nc.vector.tensor_scalar(away[:, :], keys[h][:, :], -1.0, K["spare"][:, 0:1],
                                            ALU.mult, ALU.add).then_inc(s_cnt, 1)
                    dve.wait_ge(s_cnt, q * 7 + 5)
                    nc.vector.scalar_tensor_tensor(out=step[:, :], in0=earlier[:, :], scalar=0.5,
                                                   in1=away[:, :], op0=ALU.is_gt, op1=ALU.mult
                                                   ).then_inc(s_cnt, 1)
                    dve.wait_ge(s_cnt, q * 7 + 6)
                    nc.vector.tensor_tensor(target[h][:, :], step[:, :], keys[h][:, :], ALU.add
                                            ).then_inc(s_cnt, 1)
                    dve.wait_ge(s_rows[h], (i + 1) * landed)
                    if not last:
                        stage_gather(q + 2, h)
                    if degrees:
                        if not first:
                            dve.wait_ge(s_deg, q - 1)
                        one_hot(nc, K, K["high_dst"], K["low_dst"], bass.ds(q, 1), hot_high[h], hot_low[h]
                                ).then_inc(s_hot, 1)
                    if kind == "rel":
                        nc.vector.tensor_tensor(mask[h][:, :, :],
                                                bc(K["iota"][:, 0:REL].unsqueeze(1), [P, QUAD, REL]),
                                                bc(K["rel"][:, :, q].unsqueeze(2), [P, QUAD, REL]),
                                                ALU.is_equal).then_inc(s_mask, 1)
                        dve.wait_ge(s_mask, q + 1)
                        for j in range(QUAD):
                            if not (first and h == 0):
                                dve.wait_ge(s_zt, 4 * q + j - 3)
                            nc.vector.tensor_tensor(z[j][:, :, :],
                                                    bc(rows[h][:, j, :].unsqueeze(1), [P, REL, D]),
                                                    bc(mask[h][:, j, :].unsqueeze(2), [P, REL, D]),
                                                    ALU.mult).then_inc(s_z, 1)
                    if kind == "mlp":
                        dve.wait_ge(s_p2, q + 1)
                        if not (first and h == 0):
                            dve.wait_ge(s_e2, q)
                        nc.vector.tensor_tensor(biased[:, :, :], p_2[:, :, :],
                                                bc(weights["b2"][:, :].unsqueeze(1), [P, QUAD, HID]),
                                                ALU.add).then_inc(s_b2, 1)
                    if not (first and h == 0):
                        hand_over(q - 1, 1 - h, first)

            rounds(dve, ROUNDS, body)
            hand_over(QUADS - 1, 1, False)
            if degrees:
                dve.wait_ge(s_deg, QUADS)
                nc.vector.tensor_scalar(K["dinv"][:, :], p_deg[:, 0:T], 1.0, None, ALU.add).then_inc(s_root, 1)
                dve.wait_ge(s_root, 2)
                nc.vector.reciprocal(K["dinv"][:, :], K["dinv"][:, :])

        @block.tensor
        def _(pe):
            def spread(h):
                for j in range(QUAD):
                    last = nc.tensor.matmul(p_key[h][:, j, :], bc(keys[h][:, j:j + 1], [P, P]),
                                            K["ident"][:, :], start=True, stop=True)
                last.then_inc(s_prow, 1)

            pe.wait_ge(s_keys, 1)
            spread(0)

            def body(i, first, last):
                for h in range(2):
                    q = i * 2 + h
                    if not (last and h == 1):
                        pe.wait_ge(s_keys, q + 2)
                        if not (first and h == 0):
                            pe.wait_ge(s_same, q)
                        spread(1 - h)
                    pe.wait_ge(s_rows[h], (i + 1) * landed)
                    if kind == "mlp":
                        if not (first and h == 0):
                            pe.wait_ge(s_ht, q)
                        for j in range(QUAD):
                            last_mm = flip128(nc, p_t[:, j * P:(j + 1) * P], rows[h][:, j, :],
                                                          K["ident"][:, :])
                        last_mm.then_inc(s_pt, 1)
                        pe.wait_ge(s_ht, q + 1)
                        pe.wait_ge(s_ew[h], 16 * (i + 1))
                        if not (first and h == 0):
                            pe.wait_ge(s_e1, q)
                        nc.tensor.matmul(p_1[:, :], weights["W1"][:, :], ht[:, :], start=True, stop=False)
                        nc.tensor.matmul(p_1[:, :], weights["w1d"][:, :], ew[h][:, :], start=False,
                                         stop=True).then_inc(s_p1, 1)
                        pe.wait_ge(s_e1, q + 1)
                        if not (first and h == 0):
                            pe.wait_ge(s_b2, q)
                        for j in range(QUAD):
                            last_mm = nc.tensor.matmul(p_2[:, j, :], e1[:, j * P:(j + 1) * P],
                                                       weights["W2"][:, :], start=True, stop=True)
                        last_mm.then_inc(s_p2, 1)
                        pe.wait_ge(s_e2, q + 1)
                    pe.wait_ge(s_same, q + 1)
                    if not first:
                        pe.wait_ge(s_total, q - 1)
                    if kind == "rel":
                        def finish(j):
                            pe.wait_ge(s_ztb, 4 * q + j + 1)
                            for c in range(4):
                                mm = nc.tensor.matmul(p_sum[h][:, j, 0:D], ztb[j % 2][:, c, :],
                                                      weights["W"][:, c, :], start=c == 0, stop=c == 3)
                            return mm
                        for j in range(QUAD):
                            pe.wait_ge(s_z, 4 * q + j + 1)
                            if not (first and h == 0 and j < 2):
                                pe.wait_ge(s_ztb, 4 * q + j - 1)
                            for c in range(4):
                                mm = nc.tensor.matmul(
                                    p_zt[j % 2][:, c, :],
                                    z[j][:, 2 * c:2 * c + 2, :].rearrange("p r f -> p (r f)"),
                                    same[h][:, j, :], start=True, stop=True)
                            mm.then_inc(s_zt, 1)
                            if j:
                                finish(j - 1)
                        finish(QUAD - 1).then_inc(s_sum, 1)
                    else:
                        if degrees:
                            pe.wait_ge(s_hot, q + 1)
                            for j in range(QUAD):
                                mm = nc.tensor.matmul(p_deg[:, 0:T], hot_high[h][:, j, :], hot_low[h][:, j, :],
                                                      start=first and h == 0 and j == 0,
                                                      stop=last and h == 1 and j == QUAD - 1)
                            mm.then_inc(s_deg, 1)
                        message = e2 if kind == "mlp" else rows[h]
                        for j in range(QUAD):
                            mm = nc.tensor.matmul(p_sum[h][:, j, 0:width], same[h][:, j, :],
                                                  message[:, j, :], start=True, stop=True)
                        mm.then_inc(s_sum, 1)

            rounds(pe, ROUNDS, body)

        @block.scalar
        def _(act):
            def hand_over(q, h, fresh):
                act.wait_ge(s_sum, q + 1)
                if not fresh:
                    scattered(act, q)
                nc.scalar.copy(total[h][:, :, :], p_sum[h][:, :, 0:width]).then_inc(s_total, 1)

            def body(i, first, last):
                for h in range(2):
                    q = i * 2 + h
                    if kind != "mlp" and not (first and h == 0):
                        hand_over(q - 1, 1 - h, first)
                    if kind == "rel":
                        for j in range(QUAD):
                            act.wait_ge(s_zt, 4 * q + j + 1)
                            nc.scalar.copy(ztb[j % 2][:, :, :], p_zt[j % 2][:, :, :]).then_inc(s_ztb, 1)
                    if kind == "mlp":
                        act.wait_ge(s_pt, q + 1)
                        if not (first and h == 0):
                            act.wait_ge(s_p1, q)
                        nc.scalar.copy(ht[:, :], p_t[:, :]).then_inc(s_ht, 1)
                        act.wait_ge(s_p1, q + 1)
                        if not (first and h == 0):
                            act.wait_ge(s_p2, q)
                        nc.scalar.activation(e1[:, :], p_1[:, :], ACT.Silu,
                                             bias=weights["b1"][:, 0:1]).then_inc(s_e1, 1)
                        act.wait_ge(s_b2, q + 1)
                        if not (first and h == 0):
                            act.wait_ge(s_sum, q)
                        nc.scalar.activation(e2[:, :, :], biased[:, :, :], ACT.Silu).then_inc(s_e2, 1)

            rounds(act, ROUNDS, body)
            if kind != "mlp":
                hand_over(QUADS - 1, 1, False)
            if degrees:
                act.wait_ge(s_root, 1)
                nc.scalar.activation(K["dinv"][:, :], K["dinv"][:, :], ACT.Sqrt).then_inc(s_root, 1)

        inner.close()
        clear(nc, sems)


def prepare(nc, K, src, dst, rel, x, xp, y0, sums):
    with ExitStack() as ctx:
        def sb(name, shape, dt=F32):
            return ctx.enter_context(nc.sbuf_tensor(f"pre_{name}", shape, dt))

        sems = []

        def sem(name):
            sems.append(ctx.enter_context(nc.semaphore(f"pre_{name}")))
            return sems[-1]

        lists = (("src", src, PADKEY), ("dst", dst, PADKEY), ("rel", rel, 0))
        raw = [sb(f"raw_{n}", [QUADS, QE], I32) for n, _, _ in lists]
        rawf = [sb(f"rawf_{n}", [QUADS, QE]) for n, _, _ in lists]
        high = [sb("high_src", [P, QUAD, QUADS]), K["high_dst"]]
        low = [sb("low_src", [P, QUAD, QUADS]), K["low_dst"]]
        highi = sb("highi", [P, QUAD, QUADS], I32)
        below = sb("below", [P, QUAD, QUADS])
        iotai = sb("iotai", [P, T], I32)
        iota16 = K["iota16"]
        sparei = sb("sparei", [P, 1], I32)
        hot_high = [sb(f"hot_high{h}", [P, QUAD, P], F16) for h in range(2)]
        hot_low = [sb(f"hot_low{h}", [P, QUAD, T], F16) for h in range(2)]
        xall = sb("xall", [P, T, D])
        present = sb("present", [P, T])
        threshold = sb("threshold", [P, QUAD, QUADS])
        total = sb("total", [P, T])
        count = sb("count", [P, T])
        part16 = sb("part16", [3, D], BF16)
        kept = sb("kept", [3, D])
        p_t = [ctx.enter_context(nc.psum_tensor(f"pre_p_t{k}", [P, QUAD, P], F32)) for k in range(3)]
        p_deg = ctx.enter_context(nc.psum_tensor("pre_p_deg", [P, 512], F32))
        p_step = ctx.enter_context(nc.psum_tensor("pre_p_step", [P, 512], F32))

        s_padded = sem("padded")
        s_raw = sem("raw")
        s_x = sem("x")
        s_xp = sem("xp")
        s_y = sem("y")
        s_y0 = sem("y0")
        s_zero = sem("zero")
        s_clear = sem("clear")
        s_weights = sem("weights")
        s_bias = sem("bias")
        s_blank = sem("blank")
        s_const = sem("const")
        s_edge = sem("edge")
        s_rawf = sem("rawf")
        s_pt = sem("pt")
        s_v = sem("v")
        s_hot = sem("hot")
        s_split = sem("split")
        s_steps = sem("steps")
        s_deg = sem("deg")
        s_max = sem("max")
        s_root = sem("root")
        inner = ctx.enter_context(ExitStack())
        block = inner.enter_context(nc.Block())

        @block.gpsimd
        def _(pool):
            nc.gpsimd.memset(K["ident"][:, :], 0.0).then_inc(s_const, 1)
            nc.gpsimd.memset(K["before"][:, :], 1.0).then_inc(s_const, 1)
            pool.wait_ge(s_const, 2)
            nc.gpsimd.affine_select(out=K["ident"][:, :], in_=K["ident"][:, :],
                                    compare_op=ALU.not_equal, fill=1.0, base=0, pattern=[[-1, P]],
                                    channel_multiplier=1).then_inc(s_const, 1)
            nc.gpsimd.affine_select(out=K["before"][:, :], in_=K["before"][:, :],
                                    compare_op=ALU.is_gt, fill=0.0, base=0, pattern=[[-1, P]],
                                    channel_multiplier=1).then_inc(s_const, 1)
            nc.gpsimd.iota(iotai[:, :], [[1, T]], base=0, channel_multiplier=0).then_inc(s_const, 1)
            nc.gpsimd.iota(sparei[:, :], [[1, 1]], base=NR, channel_multiplier=1).then_inc(s_const, 1)
            pool.wait_ge(s_const, 6)
            nc.gpsimd.memset(xall[96:P, LASTT:T, :], 0.0).then_inc(s_edge, 1)

        @block.sync
        def _(sp):
            sp.wait_ge(s_padded, 3)
            for n, (_, a, _) in enumerate(lists):
                sp.dma_start(raw[n][0:96, :], a[0:96 * QE].rearrange("(q e) -> q e", e=QE)).then_inc(s_raw, 16)
                sp.dma_start(raw[n][96:97, :], a[96 * QE:97 * QE].rearrange("(q e) -> q e", e=QE)).then_inc(s_raw, 16)
                sp.dma_start(raw[n][97:98, 0:RESTQ], a[97 * QE:N].rearrange("(q e) -> q e", q=1)).then_inc(s_raw, 16)
            sp.wait_ge(s_edge, 1)
            full = x[0:LASTP * T, :].rearrange("(p t) f -> p (t f)", p=LASTP)
            rows = xall[:, :, :].rearrange("p t f -> p (t f)")
            for a in range(0, T * D, XW):
                for p0, p1 in ((0, 112), (112, LASTP)):
                    sp.dma_start(rows[p0:p1, a:a + XW], full[p0:p1, a:a + XW]).then_inc(s_x, 16)
            sp.dma_start(rows[LASTP:P, 0:LASTT * D],
                         x[LASTP * T:N, :].rearrange("(a n) f -> a (n f)", a=1)).then_inc(s_x, 16)
            sp.wait_ge(s_x, 16 * (2 * XPARTS + 1))
            to = xp.rearrange("(p t) f -> p (t f)", p=P)
            for n in range(XPARTS):
                sp.dma_start(to[:, n * XW:(n + 1) * XW], rows[:, n * XW:(n + 1) * XW]).then_inc(s_xp, 16)
            sp.wait_ge(s_zero, 1)
            for table in sums:
                flat = table.rearrange("(p t) f -> p (t f)", p=P)
                for a in range(0, flat.shape[1], PIECE):
                    sp.dma_start(flat[:, a:a + PIECE], K["zero"][:, :]).then_inc(s_clear, 16)
            to = y0.rearrange("(p t) f -> p (t f)", p=P)
            for n in range(XPARTS):
                sp.wait_ge(s_y, n + 1)
                sp.dma_start(to[:, n * XW:(n + 1) * XW], rows[:, n * XW:(n + 1) * XW]).then_inc(s_y0, 16)
            sp.wait_ge(s_y0, 16 * XPARTS)
            sp.wait_ge(s_clear, 16 * len(sums) * (NA * D // P // PIECE))

        @block.vector
        def _(dve):
            for weights in K["diagonal"]:
                nc.vector.memset(weights, 0.0).then_inc(s_blank, 1)
            for n, (_, _, pad) in enumerate(lists):
                nc.vector.memset(raw[n][:, :], pad).then_inc(s_padded, 1)
            nc.vector.memset(K["zero"][:, :], 0.0).then_inc(s_zero, 1)
            nc.vector.memset(K["eps"][:, :], EPS)
            dve.wait_ge(s_raw, 16 * 9)
            for n in range(3):
                nc.vector.tensor_copy(rawf[n][:, :], raw[n][:, :]).then_inc(s_rawf, 1)
            dve.wait_ge(s_const, 6)
            nc.vector.tensor_copy(K["iota"][:, :], iotai[:, :])
            nc.vector.tensor_copy(iota16[:, :], iotai[:, :])
            nc.vector.tensor_copy(K["spare"][:, :], sparei[:, :])
            v = 0
            for n, name in enumerate(("src", "dst", "rel")):
                dve.wait_ge(s_pt, n + 1)
                nc.vector.tensor_copy(K[name][:, :, :], p_t[n][:, :, 0:QUADS]).then_inc(s_v, 1)
                v += 1
                if n < 2:
                    nc.vector.tensor_copy(K[name + "i"][:, :, :], p_t[n][:, :, 0:QUADS]).then_inc(s_v, 1)
                    v += 1
                    dve.wait_ge(s_v, v)
                    nc.vector.tensor_scalar(highi[:, :, :], K[name][:, :, :], 1.0 / T, 0.5 / T,
                                            ALU.mult, ALU.add).then_inc(s_v, 1)
                    dve.wait_ge(s_v, v + 1)
                    nc.vector.tensor_copy(high[n][:, :, :], highi[:, :, :]).then_inc(s_v, 1)
                    dve.wait_ge(s_v, v + 2)
                    nc.vector.scalar_tensor_tensor(out=low[n][:, :, :], in0=high[n][:, :, :],
                                                   scalar=float(-T), in1=K[name][:, :, :],
                                                   op0=ALU.mult, op1=ALU.add).then_inc(s_v, 1)
                    dve.wait_ge(s_v, v + 3)
                    nc.vector.tensor_scalar(below[:, :, :], low[n][:, :, :], 0.0, None, ALU.is_lt
                                            ).then_inc(s_v, 1)
                    dve.wait_ge(s_v, v + 4)
                    nc.vector.tensor_tensor(high[n][:, :, :], high[n][:, :, :], below[:, :, :],
                                            ALU.subtract).then_inc(s_v, 1)
                    nc.vector.scalar_tensor_tensor(out=low[n][:, :, :], in0=below[:, :, :],
                                                   scalar=float(T), in1=low[n][:, :, :],
                                                   op0=ALU.mult, op1=ALU.add).then_inc(s_v, 1)
                    v += 6
            dve.wait_ge(s_v, v)
            nc.vector.tensor_scalar(threshold[:, :, :], low[0][:, :, :], -1.0, 0.5, ALU.mult, ALU.add
                                    ).then_inc(s_split, 1)

            def body(i, first, last):
                for h in range(2):
                    q = i * 2 + h
                    if not first:
                        dve.wait_ge(s_deg, q - 1)
                    one_hot(nc, K, high[0], low[0], bass.ds(q, 1), hot_high[h], hot_low[h], HOTS).then_inc(s_hot, 1)

            rounds(dve, ROUNDS, body)
            dve.wait_ge(s_deg, QUADS)
            nc.vector.tensor_copy(total[:, :], p_step[:, 0:T]).then_inc(s_v, 1)
            dve.wait_ge(s_v, v + 1)
            nc.vector.tensor_tensor(count[:, 1:T], total[:, 1:T], total[:, 0:T - 1], ALU.subtract).then_inc(s_v, 1)
            nc.vector.tensor_tensor(count[:, 0:1], total[:, 0:1], total[:, T - 1:T], ALU.add).then_inc(s_v, 1)
            dve.wait_ge(s_v, v + 3)
            nc.vector.scalar_tensor_tensor(out=count[:, :], in0=count[:, :], scalar=0.5, in1=p_deg[:, 0:T],
                                           op0=ALU.mult, op1=ALU.add).then_inc(s_v, 1)
            v += 4
            dve.wait_ge(s_v, v)
            nc.vector.tensor_scalar(present[:, :], count[:, :], 0.5, None, ALU.is_gt).then_inc(s_v, 1)
            nc.vector.tensor_scalar(K["dis"][:, :], count[:, :], 1.0, None, ALU.max).then_inc(s_max, 1)
            dve.wait_ge(s_root, 1)
            nc.vector.reciprocal(K["dis"][:, :], K["dis"][:, :]).then_inc(s_v, 1)
            dve.wait_ge(s_v, v + 2)
            nc.vector.tensor_tensor(K["dis"][:, :], K["dis"][:, :], present[:, :], ALU.mult).then_inc(s_v, 1)
            dve.wait_ge(s_v, v + 3)
            dve.wait_ge(s_xp, 16 * XPARTS)
            for n in range(XPARTS):
                part = xall[:, n * XC:(n + 1) * XC, :]
                nc.vector.tensor_tensor(part, part, bc(K["dis"][:, n * XC:(n + 1) * XC].unsqueeze(2), [P, XC, D]),
                                        ALU.mult).then_inc(s_y, 1)
            wemb, biases = K["residual"], K["biases"]
            dve.wait_ge(s_weights, 16 * len(K["loads"]))
            nc.vector.tensor_tensor(wemb[:, :], wemb[:, :], K["ident"][:, :], ALU.add)
            nc.vector.memset(K["ones3"][:, :], 1.0)
            b = 0

            def step(op):
                nonlocal b
                op.then_inc(s_bias, 1)
                b += 1
                dve.wait_ge(s_bias, b)

            for parts, to in biases:
                if len(parts) > 1:
                    step(nc.vector.tensor_tensor(parts[0][:, :], parts[0][:, :], parts[1][:, :], ALU.add))
                rest = parts[0]
                for r in range(3):
                    step(nc.vector.tensor_copy(part16[:, :], rest[:, :]))
                    if r < 2:
                        step(nc.vector.tensor_tensor(rest[:, :], rest[:, :], part16[:, :], ALU.subtract))
                    if r == 0:
                        step(nc.vector.tensor_scalar(kept[:, :], part16[:, :], K["ident"][0:3, 0:1], None, ALU.mult))
                    else:
                        step(nc.vector.scalar_tensor_tensor(out=kept[:, :], in0=part16[:, :],
                                                            scalar=K["ident"][0:3, r:r + 1], in1=kept[:, :],
                                                            op0=ALU.mult, op1=ALU.add))
                step(nc.vector.tensor_copy(to[:, :, :], bc(kept[:, :].unsqueeze(1), [3, QUAD, D])))

        @block.tensor
        def _(pe):
            pe.wait_ge(s_const, 6)
            for n in range(3):
                pe.wait_ge(s_rawf, n + 1)
                for j in range(QUAD):
                    mm = flip128(nc, p_t[n][:, j, 0:QUADS], rawf[n][:, j * P:(j + 1) * P],
                                             K["ident"][0:QUADS, 0:QUADS])
                mm.then_inc(s_pt, 1)

            def body(i, first, last):
                for h in range(2):
                    q = i * 2 + h
                    pe.wait_ge(s_hot, q + 1)
                    pe.wait_ge(s_steps, q + 1)
                    for j in range(QUAD):
                        mm = nc.tensor.matmul((p_deg if j < HOTS else p_step)[:, 0:T],
                                              hot_high[h][:, j, :], hot_low[h][:, j, :],
                                              start=first and h == 0 and j in (0, HOTS),
                                              stop=last and h == 1 and j in (HOTS - 1, QUAD - 1))
                    mm.then_inc(s_deg, 1)

            rounds(pe, ROUNDS, body)

        @block.scalar
        def _(act):
            act.wait_ge(s_blank, 4)
            for to, of in K["loads"]:
                act.dma_start(to, of).then_inc(s_weights, 16)
            act.wait_ge(s_split, 1)

            def body(i, first, last):
                for h in range(2):
                    q = i * 2 + h
                    if not first:
                        act.wait_ge(s_deg, q - 1)
                    for j in range(HOTS, QUAD):
                        op = nc.scalar.activation(hot_low[h][:, j, :], K["iota16"][:, :], ACT.Sign,
                                                  bias=threshold[:, j, bass.ds(q, 1)])
                    op.then_inc(s_steps, 1)

            rounds(act, ROUNDS, body)
            act.wait_ge(s_max, 1)
            nc.scalar.activation(K["dis"][:, :], K["dis"][:, :], ACT.Sqrt).then_inc(s_root, 1)

        inner.close()
        clear(nc, sems)


def node_pass(nc, label, K, kind, ins, outs, weights=None, copy=None):
    dense = kind in ("mlp", "conv1", "conv2")
    conv = kind in ("conv1", "conv2")
    normed = kind != "conv1"
    NQ = CH // QUAD
    NS = 2 * NQ
    with ExitStack() as ctx:
        def sb(name, shape, dt=F32):
            return ctx.enter_context(nc.sbuf_tensor(f"{label}_{name}", shape, dt))

        def ps(name, shape):
            return ctx.enter_context(nc.psum_tensor(f"{label}_{name}", shape, F32))

        sems = []

        def sem(name):
            sems.append(K["semaphore"](f"node_{name}"))
            return sems[-1]

        widths = [t.shape[1] for t in ins]
        late = 1 if kind == "conv2" else 0
        early = len(ins) - late
        got = [[sb(f"in{n}_{h}", [P, CH, w]) for h in range(2)] for n, w in enumerate(widths)]
        result = [[sb(f"out{n}_{h}", [P, CH, D]) for h in range(2)] for n in range(len(outs))]
        value = [sb(f"value{h}", [P, CH, D]) for h in range(2)]
        s_in = [sem(f"in{h}") for h in range(2)]
        s_late = [sem(f"late{h}") for h in range(2)]
        s_out = [sem(f"out{h}") for h in range(2)]
        s_turn = sem("turn")
        s_tail = sem("tail")
        s_done = sem("done")
        s_v = sem("v")
        s_w = sem("w")
        s_value = sem("value")
        s_c = sem("c")
        s_sq = sem("sq")
        s_var = sem("var")
        s_std = sem("std")
        s_x3 = sem("x3")
        cent = [sb(f"cent{h}", [P, CH, D]) for h in range(2)]
        sq = sb("sq", [P, CH, D])
        mean = sb("mean", [P, CH])
        var = sb("var", [P, CH])
        std = sb("std", [P, CH])
        rstd = [sb(f"rstd{h}", [P, CH]) for h in range(2)]
        if dense:
            s_z = sem("z")
            s_pt = sem("pt")
            s_t = sem("t")
            s_p = sem("p")
            s_u = sem("u")
            s_q = sem("q")
            s_o = sem("o")
            z = [sb(f"z{h}", [P, CH, D]) for h in range(2)] if conv else None
            XQ = QE if kind == "conv2" else QE // 2
            flat_x = [sb(f"flat_x{n}", [P, XQ]) for n in range(NQ)]
            p_x = [ps(f"p_x{b}", [P, 512]) for b in range(2)]
            p_o = [ps(f"p_o{b}", [P, 2 * QUAD, D]) for b in range(2)]
            if kind == "mlp":
                flat_a = [sb(f"flat_a{n}", [P, QE]) for n in range(NQ)]
                u = [sb(f"u{b}", [P, QE]) for b in range(2)]
                p_a = [ps(f"p_a{b}", [P, QE]) for b in range(2)]
                p_1 = [ps(f"p_1{b}", [P, QE]) for b in range(2)]
        inner = ctx.enter_context(ExitStack())
        block = inner.enter_context(nc.Block())
        stores = 3 if kind == "conv2" else len(outs) + (copy is not None)

        def place(i, k):
            return i * NS + k, i * 2 + k // NQ, (k // NQ) % 2, k % 2, k % NQ

        def slot(j):
            return slice((j % 2 * 2 + j // 2) * P, (j % 2 * 2 + j // 2 + 1) * P)

        @block.sync
        def _(sp):
            def load(c, h, of, signal):
                for n in of:
                    w = widths[n]
                    sp.dma_start(got[n][h][:, :, :].rearrange("p t f -> p (t f)"),
                                 ins[n][0:NR, :].rearrange("(p t) f -> p (t f)", p=P)[:, bass.ds(c * (CH * w), CH * w)]
                                 ).then_inc(signal[h], 16)

            def store(c, h):
                sp.wait_ge(s_done, c + 1)
                for n, table in enumerate(outs):
                    of = result[n][h][:, :, :].rearrange("p t f -> p (t f)")
                    if kind != "conv2":
                        sp.dma_start(chunk_of(table, c), of).then_inc(s_out[h], 16)
                        continue
                    full, tail = table
                    to = full[0:LASTP * T, :].rearrange("(p t) f -> p (t f)", p=LASTP)
                    sp.dma_start(to[0:112, bass.ds(c * CW, CW)], of[0:112, :]).then_inc(s_out[h], 16)
                    sp.dma_start(to[112:LASTP, bass.ds(c * CW, CW)], of[112:LASTP, :]).then_inc(s_out[h], 16)
                    sp.dma_start(tail.rearrange("(a t) f -> a (t f)", a=1)[:, bass.ds(c * CW, CW)],
                                 of[LASTP:P, :]).then_inc(s_out[h], 16)
                if copy is not None:
                    sp.dma_start(chunk_of(copy, c), of).then_inc(s_out[h], 16)

            for h in range(2):
                load(h, h, range(early), s_in)
                load(h, h, range(early, len(ins)), s_late)
            if copy is not None:
                sp.dma_start(copy[NR:NA, :], K["zero"][:, 0:D]).then_inc(s_tail, 16)

            def body(i, first, last):
                for h in range(2):
                    c = i * 2 + h
                    if not last:
                        if kind == "mlp":
                            sp.wait_ge(s_o, (c + 1) * NQ)
                        elif conv:
                            sp.wait_ge(s_z, c + 1)
                        else:
                            sp.wait_ge(s_value, c + 1)
                        load(c + 2, h, range(early), s_in)
                    if not (first and h == 0):
                        store(c - 1, 1 - h)
                    if late and not last:
                        sp.wait_ge(s_pt, (c + 1) * NQ)
                        load(c + 2, h, range(early, len(ins)), s_late)

            rounds(sp, CROUNDS, body)
            store(CHUNKS - 1, 1)
            for h in range(2):
                sp.wait_ge(s_out[h], 16 * stores * CROUNDS)
            if copy is not None:
                sp.wait_ge(s_tail, 16)
            if kind == "conv2":
                full, tail = outs[0]
                sp.dma_start(full[LASTP * T:N, :].rearrange("(a n) f -> a (n f)", a=8),
                             tail[0:LASTT, :].rearrange("(a n) f -> a (n f)", a=8)).then_inc(s_tail, 16)
                sp.wait_ge(s_tail, 16)

        @block.vector
        def _(dve):
            def scale_of(name, c):
                return bc(K[name][:, bass.ds(c * CH, CH)].unsqueeze(2), [P, CH, D])

            def before(i, k, first):
                c = i * 2 + k
                h = k % 2
                g = [got[n][h][:, :, :] for n in range(early)]
                if kind == "mlp":
                    return
                dve.wait_ge(s_in[h], 16 * early * (i + k // 2 + 1))
                if kind == "norm0":
                    v = value[h][:, :, :]
                    nc.vector.tensor_tensor(v, g[1], g[2], ALU.add).then_inc(s_v, 1)
                    dve.wait_ge(s_v, 2 * c + 1)
                    nc.vector.tensor_tensor(v, v, scale_of("dis", c), ALU.mult).then_inc(s_v, 1)
                    dve.wait_ge(s_v, 2 * c + 2)
                    nc.vector.tensor_tensor(v, v, g[0], ALU.add).then_inc(s_value, 1)
                elif kind == "norm":
                    nc.vector.tensor_tensor(value[h][:, :, :], g[0], g[1], ALU.add).then_inc(s_value, 1)
                else:
                    if k >= 2:
                        dve.wait_ge(s_pt, (c - 1) * NQ)
                    v = z[h][:, :, :]
                    nc.vector.tensor_tensor(v, g[0], g[1], ALU.add).then_inc(s_v, 1)
                    dve.wait_ge(s_v, c + 1)
                    nc.vector.tensor_tensor(v, v, scale_of("dinv", c), ALU.mult).then_inc(s_z, 1)

            def means(c, h):
                nc.vector.tensor_reduce(mean[:, :], value[h][:, :, :], AX.X, ALU.add).then_inc(s_w, 1)
                dve.wait_ge(s_w, 3 * c + 1)
                nc.vector.tensor_scalar(mean[:, :], mean[:, :], 1.0 / D, None, ALU.mult).then_inc(s_w, 1)

            def center(c, h, first):
                dve.wait_ge(s_w, 3 * c + 2)
                if kind != "mlp" and not first:
                    dve.wait_ge(s_done, c - 1)
                nc.vector.tensor_tensor(cent[h][:, :, :], value[h][:, :, :],
                                        bc(mean[:, :].unsqueeze(2), [P, CH, D]), ALU.subtract).then_inc(s_c, 1)

            def variance(c):
                dve.wait_ge(s_sq, c + 1)
                nc.vector.tensor_reduce(var[:, :], sq[:, :, :], AX.X, ALU.add).then_inc(s_var, 1)

            def scale(c, h):
                dve.wait_ge(s_std, c + 1)
                nc.vector.reciprocal(rstd[h][:, :], std[:, :]).then_inc(s_w, 1)

            def norm(c, h, written):
                dve.wait_ge(s_w, 3 * c + 3)
                if written is not None:
                    dve.wait_ge(s_out[h], 16 * stores * written)
                nc.vector.tensor_tensor(result[0][h][:, :, :], cent[h][:, :, :],
                                        bc(rstd[h][:, :].unsqueeze(2), [P, CH, D]), ALU.mult).then_inc(s_x3, 1)

            def scaled(c, h):
                dve.wait_ge(s_x3, c + 1)
                nc.vector.tensor_tensor(result[1][h][:, :, :], result[0][h][:, :, :],
                                        scale_of("dinv", c), ALU.mult).then_inc(s_done, 1)

            def out_of(i, k, first):
                m, c, h, b, n = place(i, k)
                part = slice(n * QUAD, (n + 1) * QUAD)
                if n == 0:
                    dve.wait_ge(s_in[h], 16 * early * (i + 1))
                    if not first:
                        dve.wait_ge(s_c, c - 1)
                dve.wait_ge(s_q, m + 1)
                nc.vector.tensor_tensor(value[h][:, part, :], p_o[b][:, 0:QUAD, :], got[0][h][:, part, :],
                                        ALU.add).then_inc(s_o, 1)

            def finish(c, h, n, written):
                if n == 0:
                    dve.wait_ge(s_o, (c + 1) * NQ)
                    means(c, h)
                if n == 1:
                    center(c, h, True)
                if n == 3:
                    variance(c)
                if n == 5:
                    scale(c, h)
                    norm(c, h, written)
                if n == 6:
                    scaled(c, h)

            def body(i, first, last):
                if kind == "mlp":
                    for k in range(NS):
                        m, c, h, b, n = place(i, k)
                        out_of(i, k, first)
                        if h == 1:
                            finish(c - 1, 0, n, None if first else i)
                        elif not first:
                            finish(c - 1, 1, n, i - 1 if type(i) is not int or i > 1 else None)
                    return
                for h in range(2):
                    c = i * 2 + h
                    if not normed:
                        if not last:
                            before(i, h + 2, first)
                        dve.wait_ge(s_o, (c + 1) * NQ)
                        if not first:
                            dve.wait_ge(s_out[h], 16 * stores * i)
                        nc.vector.tensor_tensor(result[0][h][:, :, :], value[h][:, :, :],
                                                scale_of("dinv", c), ALU.mult).then_inc(s_done, 1)
                        continue
                    if dense:
                        dve.wait_ge(s_o, (c + 1) * NQ)
                    else:
                        dve.wait_ge(s_value, c + 1)
                    means(c, h)
                    center(c, h, first)
                    if dense and not last:
                        before(i, h + 2, first)
                    if not dense and not (last and h == 1):
                        before(i, h + 1, first)
                    variance(c)
                    scale(c, h)

            before(0, 0, True)
            if conv:
                before(0, 1, True)
            rounds(dve, CROUNDS, body, alone=2 if kind == "mlp" else 1)
            if kind == "mlp":
                for n in range(NQ):
                    finish(CHUNKS - 1, 1, n, CROUNDS - 1)

        @block.gpsimd
        def _(pool):
            if not normed:
                return

            def body(i, first, last):
                for h in range(2):
                    c = i * 2 + h
                    if kind == "mlp":
                        pool.wait_ge(s_c, c + 1)
                        pool.sem_inc(s_turn, 1)
                        nc.gpsimd.tensor_tensor(sq[:, :, :], cent[h][:, :, :], cent[h][:, :, :], ALU.mult
                                                ).then_inc(s_sq, 1)
                        continue
                    pool.wait_ge(s_w, 3 * c + 3)
                    pool.wait_ge(s_c, c + 1)
                    if not first:
                        pool.wait_ge(s_out[h], 16 * stores * i)
                    pool.sem_inc(s_turn, 1)
                    nc.gpsimd.tensor_tensor(result[0][h][:, :, :], cent[h][:, :, :],
                                            bc(rstd[h][:, :].unsqueeze(2), [P, CH, D]), ALU.mult
                                            ).then_inc(s_done, 1)

            rounds(pool, CROUNDS, body)

        @block.scalar
        def _(act):
            def square(c, h):
                if kind == "mlp":
                    return
                act.wait_ge(s_c, c + 1)
                nc.scalar.activation(sq[:, :, :], cent[h][:, :, :], ACT.Square).then_inc(s_sq, 1)

            def root(c):
                act.wait_ge(s_var, c + 1)
                nc.scalar.activation(std[:, :], var[:, :], ACT.Sqrt, scale=1.0 / D,
                                     bias=K["eps"][:, 0:1]).then_inc(s_std, 1)

            def to_sbuf(i, k, first):
                m, c, h, b, n = place(i, k)
                act.wait_ge(s_pt, m + 1)
                if not (first and k < NQ):
                    act.wait_ge(s_q, m + 1 - NQ)
                if kind == "mlp":
                    nc.scalar.copy(flat_a[n][:, :], p_a[b][:, :])
                nc.scalar.copy(flat_x[n][:, :], p_x[b][:, 0:XQ]).then_inc(s_t, 1)

            def out_of(i, k, first):
                m, c, h, b, n = place(i, k)
                act.wait_ge(s_q, m + 1)
                if n == 0 and not (first and k < NS):
                    act.wait_ge(s_c if normed else s_done, c - 1)
                nc.scalar.activation(value[h][:, n * QUAD:(n + 1) * QUAD, :], p_o[b][:, 0:QUAD, :],
                                     ACT.Relu if kind == "conv1" else ACT.Copy).then_inc(s_o, 1)

            def body(i, first, last):
                if not dense:
                    for h in range(2):
                        square(i * 2 + h, h)
                        root(i * 2 + h)
                    return
                for k in range(NS):
                    m, c, h, b, n = place(i, k)
                    if not (last and k == NS - 1):
                        to_sbuf(i, k + 1, first)
                    if kind == "mlp":
                        act.wait_ge(s_p, m + 1)
                        if not (first and k < 2):
                            act.wait_ge(s_q, m - 1)
                        nc.scalar.activation(u[b][:, :], p_1[b][:, :], ACT.Silu,
                                             bias=weights["b1"][:, 0:1]).then_inc(s_u, 1)
                    if conv and not (first and k == 0):
                        out_of(i, k - 1, first)
                    if normed and not (first and h == 0):
                        if n == (2 if kind == "mlp" else 3):
                            square(c - 1, 1 - h)
                        if n == (4 if kind == "mlp" else 6):
                            root(c - 1)

            if dense:
                to_sbuf(0, 0, True)
            rounds(act, CROUNDS, body)
            if conv:
                out_of(CROUNDS - 1, NS - 1, False)
            if dense and normed:
                square(CHUNKS - 1, 1)
                root(CHUNKS - 1)

        @block.tensor
        def _(pe):
            if not dense:
                return

            def flip(i, k, first):
                m, c, h, b, n = place(i, k)
                if n == 0:
                    if kind == "mlp":
                        pe.wait_ge(s_in[h], 16 * early * (i + k // NS + 1))
                    if late:
                        pe.wait_ge(s_late[h], 16 * late * (i + k // NS + 1))
                    if conv:
                        pe.wait_ge(s_z, c + 1)
                if not (first and k < 2):
                    pe.wait_ge(s_t, m - 1)
                pe.sem_inc(s_turn, 1)
                for j in range(0, QUAD, 2):
                    t = n * QUAD + j
                    of = z if conv else got[0]
                    mm = flip128(nc, p_x[b][:, j // 2 * P:(j // 2 + 1) * P],
                                 of[h][:, t:t + 2, :].rearrange("p t f -> p (t f)"), K["ident"][:, :])
                    if kind == "conv2":
                        mm = flip128(nc, p_x[b][:, (2 + j // 2) * P:(3 + j // 2) * P],
                                     got[early][h][:, t:t + 2, :].rearrange("p t f -> p (t f)"), K["ident"][:, :])
                    if kind == "mlp":
                        for jj in (j, j + 1):
                            mm = flip128(nc, p_a[b][:, slot(jj)], got[1][h][:, n * QUAD + jj, :], K["ident"][:, :])
                mm.then_inc(s_pt, 1)

            def first_product(i, k, first):
                m, c, h, b, n = place(i, k)
                pe.wait_ge(s_t, m + 1)
                if not (first and k < 2):
                    pe.wait_ge(s_u, m - 1)
                nc.tensor.matmul(p_1[b][:, :], weights["Wa"][:, :], flat_a[n][:, :], start=True, stop=False)
                for e in range(2):
                    mm = nc.tensor.matmul(p_1[b][:, e * 2 * P:(e + 1) * 2 * P],
                                          weights["Wx"][:, e, :], flat_x[n][:, :],
                                          start=False, stop=e == 1)
                mm.then_inc(s_p, 1)

            def second_product(i, k, first):
                m, c, h, b, n = place(i, k)
                pe.wait_ge(s_u if kind == "mlp" else s_t, m + 1)
                if not (first and k < 2):
                    pe.wait_ge(s_o, m - 1)
                nc.tensor.matmul(p_o[b][:, 0:QUAD, :], K["ones3"][:, :], weights["b"][:, :, :],
                                 start=True, stop=False)
                if conv:
                    for j in range(0, QUAD, 2):
                        for r, W in enumerate(weights["W"]):
                            mm = nc.tensor.matmul(p_o[b][:, j:j + 2, :],
                                                  flat_x[n][:, (2 * r + j // 2) * P:(2 * r + j // 2 + 1) * P],
                                                  W[:, :], start=False,
                                                  stop=j == QUAD - 2 and r == len(weights["W"]) - 1)
                else:
                    for j in range(QUAD):
                        mm = nc.tensor.matmul(p_o[b][:, j, :], u[b][:, slot(j)], weights["W"][:, :],
                                              start=False, stop=j == QUAD - 1)
                mm.then_inc(s_q, 1)

            def body(i, first, last):
                for k in range(NS):
                    if not (last and k == NS - 1):
                        flip(i, k + 1, first)
                    if kind == "mlp":
                        first_product(i, k, first)
                        if not (first and k == 0):
                            second_product(i, k - 1, first)
                    else:
                        second_product(i, k, first)

            flip(0, 0, True)
            rounds(pe, CROUNDS, body)
            if kind == "mlp":
                second_product(CROUNDS - 1, NS - 1, False)

        inner.close()
        clear(nc, sems)


def gnn(nc, x, src, dst, rel, ew, W, eW1, eb1, eW2, eb2, nW1, nb1, nW2, nb2, W1, b1, W2, b2, We, be, out):
    def table(name, rows=NR, width=D):
        return nc.dram_tensor(name, [rows, width], F32, kind="Internal").ap()

    xp = table("x_padded")
    y0 = table("y0")
    x1 = table("x1")
    x2 = table("x2")
    x3 = table("x3")
    y3 = table("y3")
    y4 = table("y4")
    tail = table("out_tail", T)
    sums0 = [table(f"sums0_{n}", NA) for n in range(2)]
    sums1 = [table(f"sums1_{n}", NA) for n in range(2)]
    sums2 = [table("sums2", NA, HID)]
    sums3 = [table(f"sums3_{n}", NA) for n in range(2)]
    sums4 = [table(f"sums4_{n}", NA) for n in range(2)]
    with ExitStack() as ctx:
        def sb(name, shape, dt=F32):
            return ctx.enter_context(nc.sbuf_tensor(name, shape, dt))

        K = {name: sb(name, shape) for name, shape in (
            ("ident", [P, P]), ("before", [P, P]), ("iota", [P, T]), ("spare", [P, 1]), ("eps", [P, 1]),
            ("src", [P, QUAD, QUADS]), ("dst", [P, QUAD, QUADS]),
            ("rel", [P, QUAD, QUADS]), ("dis", [P, T]), ("dinv", [P, T]), ("zero", [P, PIECE]))}
        semaphores = {}

        def semaphore(name):
            if name not in semaphores:
                semaphores[name] = ctx.enter_context(nc.semaphore(name))
            return semaphores[name]

        K["semaphore"] = semaphore
        K["iota16"] = sb("iota16", [P, T], F16)
        K["high_dst"] = sb("high_dst", [P, QUAD, QUADS])
        K["low_dst"] = sb("low_dst", [P, QUAD, QUADS])
        K["srci"] = sb("srci", [P, QUAD, QUADS], I32)
        K["dsti"] = sb("dsti", [P, QUAD, QUADS], I32)
        wrel = sb("wrel", [P, 4, D])
        we1 = sb("we1", [P, HID])
        we1d = sb("we1d", [1, HID])
        we2 = sb("we2", [P, HID])
        be1 = sb("be1", [P, 1])
        be2 = sb("be2", [P, HID])
        wnx = sb("wnx", [P, 2, HID])
        wna = sb("wna", [HID, HID])
        wn2 = sb("wn2", [HID, D])
        bn1 = sb("bn1", [P, 1])
        w1 = sb("w1", [P, P])
        w2 = sb("w2", [P, P])
        wemb = sb("wemb", [P, P])
        bias = {name: sb(f"bias_{name}", [3, D]) for name in ("n2", "1", "2", "emb")}
        bias16 = {name: sb(f"bias16_{name}", [3, QUAD, D], BF16) for name in ("n2", "1", "2")}
        K["ones3"] = sb("ones3", [3, P], BF16)
        K["diagonal"] = (w1[:, :], w2[:, :], wemb[:, :], wnx[:, :, :])
        K["residual"] = wemb
        K["biases"] = (((bias["n2"],), bias16["n2"]), ((bias["1"],), bias16["1"]),
                       ((bias["2"], bias["emb"]), bias16["2"]))

        def column(a):
            return a.rearrange("(n a) -> n a", a=1)

        loads = ((wrel[:, :, :], W.rearrange("(c r) i h -> (r i) c h", r=2)), (we1[:, :], eW1[0:2 * D, :]),
                 (we1d[:, :], eW1[2 * D:2 * D + 1, :]), (we2[:, :], eW2), (be1[:, :], column(eb1)),
                 (be2[:, :], eb2.partition_broadcast(P)), (wnx[0:D, 0, :], nW1[0:D, :]), (wnx[D:P, 1, :], nW1[0:D, :]),
                 (wna[:, :], nW1[D:D + HID, :]), (wn2[:, :], nW2), (bn1[:, :], column(nb1)),
                 (w1[0:D, 0:D], W1), (w1[D:P, D:P], W1), (w2[0:D, 0:D], W2), (w2[D:P, D:P], W2),
                 (wemb[0:D, 0:D], We), (wemb[D:P, D:P], We),
                 (bias["n2"][:, :], nb2.partition_broadcast(3)), (bias["1"][:, :], b1.partition_broadcast(3)),
                 (bias["2"][:, :], b2.partition_broadcast(3)), (bias["emb"][:, :], be.partition_broadcast(3)))
        K["loads"] = loads

        prepare(nc, K, src, dst, rel, x, xp, y0, sums0)
        edge_pass(nc, "e0", K, [(y0, K["dsti"])], K["src"], sums0, D, "plain", zero=sums1[1:], degrees=True)
        node_pass(nc, "n1", K, "norm0", [xp] + sums0, [x1], copy=sums1[0])
        edge_pass(nc, "e1", K, [(x1, K["srci"])], K["dst"], sums1, D, "rel", zero=sums2, weights={"W": wrel})
        node_pass(nc, "n2", K, "norm", sums1, [x2])
        edge_pass(nc, "e2", K, [(x2, K["srci"]), (x2, K["dsti"])], K["src"], sums2, HID, "mlp",
                  zero=sums3[1:],
                  weights={"W1": we1, "w1d": we1d, "W2": we2, "b1": be1, "b2": be2, "ew": ew})
        node_pass(nc, "n3", K, "mlp", [x2] + sums2, [x3, y3], copy=sums3[0],
                  weights={"Wx": wnx, "Wa": wna, "b1": bn1, "W": wn2, "b": bias16["n2"]})
        edge_pass(nc, "e3", K, [(y3, K["srci"])], K["dst"], sums3, D, "plain", zero=sums4[1:])
        node_pass(nc, "n4", K, "conv1", sums3, [y4], copy=sums4[0], weights={"W": [w1], "b": bias16["1"]})
        edge_pass(nc, "e4", K, [(y4, K["srci"])], K["dst"], sums4, D, "plain")
        node_pass(nc, "n5", K, "conv2", sums4 + [x3], [(out, tail)], weights={"W": [w2, wemb], "b": bias16["2"]})


_INS = ["x", "src", "dst", "edge_type_8", "edge_weight1", "L1_gnn_W", "L2_gnn_eW1", "L2_gnn_eb1",
        "L2_gnn_eW2", "L2_gnn_eb2", "L2_gnn_nW1", "L2_gnn_nb1", "L2_gnn_nW2", "L2_gnn_nb2",
        "L3_gnn_W1", "L3_gnn_b1", "L3_gnn_W2", "L3_gnn_b2", "L3_gnn_W_emb", "L3_gnn_b_emb"]


def kernel(**inputs):
    import numpy as _np
    import concourse.bacc as _bacc
    from concourse import mybir as _mybir
    from concourse.bass_utils import run_bass_kernel_spmd as _run

    nc = _bacc.Bacc("TRN2", target_bir_lowering=False, num_devices=1)
    arrays, args = {}, []
    for name in _INS:
        a = _np.ascontiguousarray(inputs[name])
        if name == "edge_weight1":
            a = a.reshape(-1)
        arrays[f"in_{name}"] = a
        args.append(nc.dram_tensor(f"in_{name}", a.shape, _mybir.dt.from_np(a.dtype), kind="ExternalInput").ap())
    args.append(nc.dram_tensor("out_x", (N, D), F32, kind="ExternalOutput").ap())
    gnn(nc, *args)
    r = _run(nc, [arrays], core_ids=[0])
    return r.results[0]["out_x"]
```
